# Optimizing a Trainium2 kernel written in Bass

```python
import numpy as np
import jax
import jax.numpy as jnp

def _softmax(x, axis=-1):
    return jax.nn.softmax(x, axis=axis)

def _gelu(x):
    return jax.nn.gelu(x, approximate=True)

def _silu(x):
    return jax.nn.silu(x)

def _sigmoid(x):
    return jax.nn.sigmoid(x)

def _layernorm(x, axis=-1, eps=1e-05):
    m = jnp.mean(x, axis=axis, keepdims=True)
    v = jnp.var(x, axis=axis, keepdims=True)
    return (x - m) / jnp.sqrt(v + eps)

def _scatter_add(tgt, idx, src, axis=0):
    return tgt.at[idx].add(src)

def _segment_sum(src, seg, n):
    return jax.ops.segment_sum(src, seg, n)
kernel_name = 'mk_xattn_seq_d4_seqx_r4_a7e5f8'

def setup_inputs(seed: int=0):
    np.random.seed(seed)
    _w = jnp.asarray

    def _rec_inputs():
        import jax
        import jax.numpy as jnp
        _rk = jax.random.key(seed)
        x = 7.22e-05 + 1 * jax.random.normal(jax.random.fold_in(_rk, 1), (16, 128, 256), jnp.float32)
        _lenS = 128 - jax.random.randint(jax.random.fold_in(_rk, 7), (16,), 0, max(1, 128 // 4) + 1, jnp.int32)
        _lenS2 = 128 - jax.random.randint(jax.random.fold_in(_rk, 8), (16,), 0, max(1, 128 // 4) + 1, jnp.int32)
        _ctx_1024P = jax.random.normal(jax.random.fold_in(_rk, 11), (16, 16, 256), jnp.float32)
        _ctx_1024c = jax.random.dirichlet(jax.random.fold_in(_rk, 511), 0.3 * jnp.ones((16,), jnp.float32), (16, 128))
        _ctx_1024t = jnp.einsum('bsk,bkd->bsd', _ctx_1024c, _ctx_1024P)
        _ctx_1024t = _ctx_1024t * jax.lax.rsqrt(jnp.mean(jnp.square(_ctx_1024t)) + 1e-12) * 0.953939
        ctx_1024 = 4.13588e-05 + 0.999923 * (_ctx_1024t + 0.3 * jax.random.normal(jax.random.fold_in(_rk, 611), (16, 128, 256), jnp.float32))
        itok_BxS2_4_31999 = jax.random.randint(jax.random.fold_in(_rk, 13), (16, 128), 4, 8000, jnp.int32)
        _ctxb_2048x64P = jax.random.normal(jax.random.fold_in(_rk, 14), (16, 16, 64), jnp.float32)
        _ctxb_2048x64c = jax.random.dirichlet(jax.random.fold_in(_rk, 514), 0.3 * jnp.ones((16,), jnp.float32), (16, 128))
        _ctxb_2048x64t = jnp.einsum('bsk,bkd->bsd', _ctxb_2048x64c, _ctxb_2048x64P)
        _ctxb_2048x64t = _ctxb_2048x64t * jax.lax.rsqrt(jnp.mean(jnp.square(_ctxb_2048x64t)) + 1e-12) * 0.953939
        ctxb_2048x64 = 0.50053 + 0.288505 * (_ctxb_2048x64t + 0.3 * jax.random.normal(jax.random.fold_in(_rk, 614), (16, 128, 64), jnp.float32))
        _validS = jnp.arange(128)[None, :] < _lenS[:, None]
        _validS2 = jnp.arange(128)[None, :] < _lenS2[:, None]
        _causal = jnp.tril(jnp.ones((128, 128), dtype=bool))
        mask_BxSxS2_fk0 = jnp.where(jnp.broadcast_to(_validS2[:, None, :], (16, 128, 128)), 0.0, 1.0).astype(jnp.float32)
        return (x, ctx_1024, itok_BxS2_4_31999, ctxb_2048x64, mask_BxSxS2_fk0)
    x, ctx_1024, itok_BxS2_4_31999, ctxb_2048x64, mask_BxSxS2_fk0 = _rec_inputs()

    def _L0_xattn_setup():
        import jax, jax.numpy as jnp
        import numpy as np
        import math
        B, S, D, H, FF = (4, 512, 256, 16, 1024)
        HD = D // H
        EPS = 1e-05

        def _layer_norm(x, g, b):
            m = jnp.mean(x, axis=-1, keepdims=True)
            v = jnp.mean((x - m) ** 2, axis=-1, keepdims=True)
            return (x - m) * jax.lax.rsqrt(v + EPS) * g + b

        def _self_attn(x, mask, Wq, bq, Wk, bk, Wv, bv, Wo, bo):
            b, s, d = x.shape
            q = (x @ Wq.T + bq).reshape(b, s, H, HD)
            k = (x @ Wk.T + bk).reshape(b, s, H, HD)
            v = (x @ Wv.T + bv).reshape(b, s, H, HD)
            score = jnp.einsum('bshd,bthd->bhst', q, k) / math.sqrt(HD)
            score = score + (1.0 - mask[:, None, :, :]) * -1000000000.0
            p = jax.nn.softmax(score, axis=-1)
            o = jnp.einsum('bhst,bthd->bshd', p, v).reshape(b, s, d)
            return o @ Wo.T + bo
        key = jax.random.key(seed)
        ks = jax.random.split(key, 16)
        sd = 0.02
        inp = {'tgt': jax.random.normal(ks[0], (B, S, D), jnp.float32), 'memory': jax.random.normal(ks[1], (B, S, D), jnp.float32), 'mask': jnp.broadcast_to(jnp.tril(jnp.ones((S, S), jnp.float32)), (B, S, S)), 'Wq': jax.random.normal(ks[2], (D, D), jnp.float32) * sd, 'bq': jnp.zeros((D,), jnp.float32), 'Wk': jax.random.normal(ks[3], (D, D), jnp.float32) * sd, 'bk': jnp.zeros((D,), jnp.float32), 'Wv': jax.random.normal(ks[4], (D, D), jnp.float32) * sd, 'bv': jnp.zeros((D,), jnp.float32), 'Wo': jax.random.normal(ks[5], (D, D), jnp.float32) * sd, 'bo': jnp.zeros((D,), jnp.float32), 'Wg': jax.random.normal(ks[6], (D, D), jnp.float32) * sd, 'bg': jnp.zeros((D,), jnp.float32), 'W1': jax.random.normal(ks[7], (FF, D), jnp.float32) * sd, 'b1': jnp.zeros((FF,), jnp.float32), 'W2': jax.random.normal(ks[8], (D, FF), jnp.float32) * sd, 'b2': jnp.zeros((D,), jnp.float32), 'g1': jnp.ones((D,), jnp.float32), 'be1': jnp.zeros((D,), jnp.float32), 'g2': jnp.ones((D,), jnp.float32), 'be2': jnp.zeros((D,), jnp.float32)}
        return inp
    _L0_xattn_all = _L0_xattn_setup()
    _L0_xattn_in = {k: v for k, v in _L0_xattn_all.items() if k in ('Wq', 'bq', 'Wk', 'bk', 'Wv', 'bv', 'Wo', 'bo', 'Wg', 'bg', 'W1', 'b1', 'W2', 'b2', 'g1', 'be1', 'g2', 'be2')}
    del _L0_xattn_all

    def _L1_xattn_setup():
        import jax, jax.numpy as jnp
        import numpy as np
        EMBED_DIM = 256
        LN_EPS = 1e-05

        def _layernorm(x, w, b):
            m = jnp.mean(x, axis=-1, keepdims=True)
            v = jnp.mean(jnp.square(x - m), axis=-1, keepdims=True)
            return (x - m) * jax.lax.rsqrt(v + LN_EPS) * w + b

        def _attention(q, k, v, scale):
            scores = jnp.einsum('bqd,bkd->bqk', q, k) * scale
            probs = jax.nn.softmax(scores, axis=-1)
            return jnp.einsum('bqk,bkd->bqd', probs, v)
        key = jax.random.key(seed)
        ks = jax.random.split(key, 16)
        B, SQ, SK, D, H = (8, 577, 13271, EMBED_DIM, 4)
        return {'input_features': jax.random.normal(ks[0], (B, SK, D), jnp.float32), 'query_feature': jax.random.normal(ks[1], (B, SQ, D), jnp.float32), 'norm1_w': jax.random.uniform(ks[2], (D,), jnp.float32, 0.5, 1.5), 'norm1_b': jax.random.normal(ks[3], (D,), jnp.float32) * 0.1, 'norm2_w': jax.random.uniform(ks[4], (D,), jnp.float32, 0.5, 1.5), 'norm2_b': jax.random.normal(ks[5], (D,), jnp.float32) * 0.1, 'norm3_w': jax.random.uniform(ks[6], (D,), jnp.float32, 0.5, 1.5), 'norm3_b': jax.random.normal(ks[7], (D,), jnp.float32) * 0.1, 'gamma1': jax.random.uniform(ks[8], (D,), jnp.float32, 0.5, 1.5), 'gamma2': jax.random.uniform(ks[9], (D,), jnp.float32, 0.5, 1.5), 'fc1_w': jax.random.normal(ks[10], (H, D), jnp.float32) * (1.0 / np.sqrt(D)), 'fc1_b': jax.random.normal(ks[11], (H,), jnp.float32) * 0.01, 'fc2_w': jax.random.normal(ks[12], (D, H), jnp.float32) * (1.0 / np.sqrt(H)), 'fc2_b': jax.random.normal(ks[13], (D,), jnp.float32) * 0.01}
    _L1_xattn_all = _L1_xattn_setup()
    _L1_xattn_in = {k: v for k, v in _L1_xattn_all.items() if k in ('norm1_w', 'norm1_b', 'norm2_w', 'norm2_b', 'norm3_w', 'norm3_b', 'gamma1', 'gamma2', 'fc1_w', 'fc1_b', 'fc2_w', 'fc2_b')}
    del _L1_xattn_all

    def _L2_xattn_setup():
        import jax, jax.numpy as jnp
        import numpy as np
        B, S, D_MODEL, H, D_FF = (2, 512, 256, 16, 1024)
        D_HEAD = D_MODEL // H
        LN_EPS = 1e-05

        def _xavier(key, shape):
            fan_out, fan_in = shape
            std = (2.0 / (fan_in + fan_out)) ** 0.5
            return jax.random.normal(key, shape, dtype=jnp.float32) * std

        def _layer_norm(x, g, b):
            mu = jnp.mean(x, axis=-1, keepdims=True)
            var = jnp.mean((x - mu) ** 2, axis=-1, keepdims=True)
            return (x - mu) * jax.lax.rsqrt(var + LN_EPS) * g + b
        key = jax.random.key(seed)
        ks = jax.random.split(key, 8)
        return {'q': jax.random.normal(ks[0], (B, S, D_MODEL), dtype=jnp.float32), 'k': jax.random.normal(ks[1], (B, S, D_MODEL), dtype=jnp.float32), 'Wq': _xavier(ks[2], (D_MODEL, D_MODEL)), 'bq': jnp.zeros((D_MODEL,), jnp.float32), 'Wk': _xavier(ks[3], (D_MODEL, D_MODEL)), 'bk': jnp.zeros((D_MODEL,), jnp.float32), 'Wv': _xavier(ks[4], (D_MODEL, D_MODEL)), 'bv': jnp.zeros((D_MODEL,), jnp.float32), 'W1': _xavier(ks[5], (D_FF, D_MODEL)), 'b1': jnp.zeros((D_FF,), jnp.float32), 'W2': _xavier(ks[6], (D_MODEL, D_FF)), 'b2': jnp.zeros((D_MODEL,), jnp.float32), 'ln_g': jnp.ones((D_MODEL,), jnp.float32), 'ln_b': jnp.zeros((D_MODEL,), jnp.float32), 'use_causal_mask': 1}
    _L2_xattn_all = _L2_xattn_setup()
    _L2_xattn_in = {k: v for k, v in _L2_xattn_all.items() if k in ('Wq', 'bq', 'Wk', 'bk', 'Wv', 'bv', 'W1', 'b1', 'W2', 'b2', 'ln_g', 'ln_b')}
    del _L2_xattn_all

    def _L3_xattn_setup():
        import jax, jax.numpy as jnp
        import numpy as np
        BATCH, T, H, S, P, NH = (4, 512, 256, 64, 64, 8)
        HD = H // NH

        def _layernorm(x, g, b):
            mu = jnp.mean(x, axis=-1, keepdims=True)
            var = jnp.mean((x - mu) ** 2, axis=-1, keepdims=True)
            return (x - mu) * jax.lax.rsqrt(var + 1e-05) * g + b

        def _mha(q_in, kv_in, W_qkv, b_qkv, W_o, b_o):
            Wq, Wk, Wv = jnp.split(W_qkv, 3, axis=0)
            bq, bk, bv = jnp.split(b_qkv, 3, axis=0)

            def heads(x, W, b):
                y = x @ W.T + b
                return y.reshape(y.shape[0], y.shape[1], NH, HD).transpose(0, 2, 1, 3)
            q, k, v = (heads(q_in, Wq, bq), heads(kv_in, Wk, bk), heads(kv_in, Wv, bv))
            scores = jnp.einsum('bhqd,bhkd->bhqk', q, k) * (1.0 / np.sqrt(HD))
            attn = jax.nn.softmax(scores, axis=-1)
            out = jnp.einsum('bhqk,bhkd->bhqd', attn, v)
            out = out.transpose(0, 2, 1, 3).reshape(q_in.shape)
            return out @ W_o.T + b_o
        key = jax.random.key(seed)
        ks = jax.random.split(key, 16)
        sH = 1.0 / np.sqrt(H)
        d = {}
        d['builder_state'] = jax.random.normal(ks[0], (BATCH, T, H), jnp.float32)
        d['base_state'] = jax.random.normal(ks[1], (BATCH, T, H), jnp.float32)
        d['input_ids'] = jax.random.randint(ks[2], (BATCH, T), 0, 8000)
        d['program_probs'] = jax.random.uniform(ks[3], (BATCH, T, P), jnp.float32)
        d['A'] = jax.random.normal(ks[4], (S, S), jnp.float32) * (0.5 / np.sqrt(S))
        d['Bmat'] = jax.random.normal(ks[5], (H, S), jnp.float32) * sH
        d['Cmat'] = jax.random.normal(ks[6], (S, H), jnp.float32) * (1.0 / np.sqrt(S))
        d['W_in'] = jax.random.normal(ks[7], (H, H), jnp.float32) * sH
        d['b_in'] = jnp.zeros((H,), jnp.float32)
        d['W_qkv'] = jax.random.normal(ks[8], (3 * H, H), jnp.float32) * sH
        d['b_qkv'] = jnp.zeros((3 * H,), jnp.float32)
        d['W_o'] = jax.random.normal(ks[9], (H, H), jnp.float32) * sH
        d['b_o'] = jnp.zeros((H,), jnp.float32)
        d['W_prog'] = jax.random.normal(ks[10], (H, P), jnp.float32) * (1.0 / np.sqrt(P))
        d['b_prog'] = jnp.zeros((H,), jnp.float32)
        d['g1'] = jnp.ones((H,), jnp.float32)
        d['beta1'] = jnp.zeros((H,), jnp.float32)
        d['g2'] = jnp.ones((H,), jnp.float32)
        d['beta2'] = jnp.zeros((H,), jnp.float32)
        return d
    _L3_xattn_all = _L3_xattn_setup()
    _L3_xattn_in = {k: v for k, v in _L3_xattn_all.items() if k in ('A', 'Bmat', 'Cmat', 'W_in', 'b_in', 'W_qkv', 'b_qkv', 'W_o', 'b_o', 'W_prog', 'b_prog', 'g1', 'beta1', 'g2', 'beta2')}
    del _L3_xattn_all
    return {'x': x, 'ctx_1024': ctx_1024, 'itok_BxS2_4_31999': itok_BxS2_4_31999, 'ctxb_2048x64': ctxb_2048x64, 'mask_BxSxS2_fk0': mask_BxSxS2_fk0, 'L0_xattn_Wq': _L0_xattn_in['Wq'], 'L0_xattn_bq': _L0_xattn_in['bq'], 'L0_xattn_Wk': _L0_xattn_in['Wk'], 'L0_xattn_bk': _L0_xattn_in['bk'], 'L0_xattn_Wv': _L0_xattn_in['Wv'], 'L0_xattn_bv': _L0_xattn_in['bv'], 'L0_xattn_Wo': _L0_xattn_in['Wo'], 'L0_xattn_bo': _L0_xattn_in['bo'], 'L0_xattn_Wg': _L0_xattn_in['Wg'], 'L0_xattn_bg': _L0_xattn_in['bg'], 'L0_xattn_W1': _L0_xattn_in['W1'], 'L0_xattn_b1': _L0_xattn_in['b1'], 'L0_xattn_W2': _L0_xattn_in['W2'], 'L0_xattn_b2': _L0_xattn_in['b2'], 'L0_xattn_g1': _L0_xattn_in['g1'], 'L0_xattn_be1': _L0_xattn_in['be1'], 'L0_xattn_g2': _L0_xattn_in['g2'], 'L0_xattn_be2': _L0_xattn_in['be2'], 'L1_xattn_norm1_w': _L1_xattn_in['norm1_w'], 'L1_xattn_norm1_b': _L1_xattn_in['norm1_b'], 'L1_xattn_norm2_w': _L1_xattn_in['norm2_w'], 'L1_xattn_norm2_b': _L1_xattn_in['norm2_b'], 'L1_xattn_norm3_w': _L1_xattn_in['norm3_w'], 'L1_xattn_norm3_b': _L1_xattn_in['norm3_b'], 'L1_xattn_gamma1': _L1_xattn_in['gamma1'], 'L1_xattn_gamma2': _L1_xattn_in['gamma2'], 'L1_xattn_fc1_w': _L1_xattn_in['fc1_w'], 'L1_xattn_fc1_b': _L1_xattn_in['fc1_b'], 'L1_xattn_fc2_w': _L1_xattn_in['fc2_w'], 'L1_xattn_fc2_b': _L1_xattn_in['fc2_b'], 'L2_xattn_Wq': _L2_xattn_in['Wq'], 'L2_xattn_bq': _L2_xattn_in['bq'], 'L2_xattn_Wk': _L2_xattn_in['Wk'], 'L2_xattn_bk': _L2_xattn_in['bk'], 'L2_xattn_Wv': _L2_xattn_in['Wv'], 'L2_xattn_bv': _L2_xattn_in['bv'], 'L2_xattn_W1': _L2_xattn_in['W1'], 'L2_xattn_b1': _L2_xattn_in['b1'], 'L2_xattn_W2': _L2_xattn_in['W2'], 'L2_xattn_b2': _L2_xattn_in['b2'], 'L2_xattn_ln_g': _L2_xattn_in['ln_g'], 'L2_xattn_ln_b': _L2_xattn_in['ln_b'], 'L3_xattn_A': _L3_xattn_in['A'], 'L3_xattn_Bmat': _L3_xattn_in['Bmat'], 'L3_xattn_Cmat': _L3_xattn_in['Cmat'], 'L3_xattn_W_in': _L3_xattn_in['W_in'], 'L3_xattn_b_in': _L3_xattn_in['b_in'], 'L3_xattn_W_qkv': _L3_xattn_in['W_qkv'], 'L3_xattn_b_qkv': _L3_xattn_in['b_qkv'], 'L3_xattn_W_o': _L3_xattn_in['W_o'], 'L3_xattn_b_o': _L3_xattn_in['b_o'], 'L3_xattn_W_prog': _L3_xattn_in['W_prog'], 'L3_xattn_b_prog': _L3_xattn_in['b_prog'], 'L3_xattn_g1': _L3_xattn_in['g1'], 'L3_xattn_beta1': _L3_xattn_in['beta1'], 'L3_xattn_g2': _L3_xattn_in['g2'], 'L3_xattn_beta2': _L3_xattn_in['beta2']}

def reference(x, ctx_1024, itok_BxS2_4_31999, ctxb_2048x64, mask_BxSxS2_fk0, L0_xattn_Wq, L0_xattn_bq, L0_xattn_Wk, L0_xattn_bk, L0_xattn_Wv, L0_xattn_bv, L0_xattn_Wo, L0_xattn_bo, L0_xattn_Wg, L0_xattn_bg, L0_xattn_W1, L0_xattn_b1, L0_xattn_W2, L0_xattn_b2, L0_xattn_g1, L0_xattn_be1, L0_xattn_g2, L0_xattn_be2, L1_xattn_norm1_w, L1_xattn_norm1_b, L1_xattn_norm2_w, L1_xattn_norm2_b, L1_xattn_norm3_w, L1_xattn_norm3_b, L1_xattn_gamma1, L1_xattn_gamma2, L1_xattn_fc1_w, L1_xattn_fc1_b, L1_xattn_fc2_w, L1_xattn_fc2_b, L2_xattn_Wq, L2_xattn_bq, L2_xattn_Wk, L2_xattn_bk, L2_xattn_Wv, L2_xattn_bv, L2_xattn_W1, L2_xattn_b1, L2_xattn_W2, L2_xattn_b2, L2_xattn_ln_g, L2_xattn_ln_b, L3_xattn_A, L3_xattn_Bmat, L3_xattn_Cmat, L3_xattn_W_in, L3_xattn_b_in, L3_xattn_W_qkv, L3_xattn_b_qkv, L3_xattn_W_o, L3_xattn_b_o, L3_xattn_W_prog, L3_xattn_b_prog, L3_xattn_g1, L3_xattn_beta1, L3_xattn_g2, L3_xattn_beta2):
    import jax
    import jax.numpy as jnp

    def _L0_xattn_ref(tgt, memory, mask, Wq, bq, Wk, bk, Wv, bv, Wo, bo, Wg, bg, W1, b1, W2, b2, g1, be1, g2, be2):
        import jax, jax.numpy as jnp
        import numpy as np
        import math
        B, S, D, H, FF = (4, 512, 256, 16, 1024)
        HD = D // H
        EPS = 1e-05

        def _layer_norm(x, g, b):
            m = jnp.mean(x, axis=-1, keepdims=True)
            v = jnp.mean((x - m) ** 2, axis=-1, keepdims=True)
            return (x - m) * jax.lax.rsqrt(v + EPS) * g + b

        def _self_attn(x, mask, Wq, bq, Wk, bk, Wv, bv, Wo, bo):
            b, s, d = x.shape
            q = (x @ Wq.T + bq).reshape(b, s, H, HD)
            k = (x @ Wk.T + bk).reshape(b, s, H, HD)
            v = (x @ Wv.T + bv).reshape(b, s, H, HD)
            score = jnp.einsum('bshd,bthd->bhst', q, k) / math.sqrt(HD)
            score = score + (1.0 - mask[:, None, :, :]) * -1000000000.0
            p = jax.nn.softmax(score, axis=-1)
            o = jnp.einsum('bhst,bthd->bshd', p, v).reshape(b, s, d)
            return o @ Wo.T + bo
        tgt1 = _layer_norm(tgt, g1, be1)
        tgt = tgt + _self_attn(tgt1, mask, Wq, bq, Wk, bk, Wv, bv, Wo, bo)
        tgt = tgt + (memory @ Wg.T + bg)
        tgt1 = _layer_norm(tgt, g2, be2)
        ff = jax.nn.relu(tgt1 @ W1.T + b1) @ W2.T + b2
        return tgt + ff

    def _L1_xattn_ref(input_features, query_feature, norm1_w, norm1_b, norm2_w, norm2_b, norm3_w, norm3_b, gamma1, gamma2, fc1_w, fc1_b, fc2_w, fc2_b):
        import jax, jax.numpy as jnp
        import numpy as np
        EMBED_DIM = 256
        LN_EPS = 1e-05

        def _layernorm(x, w, b):
            m = jnp.mean(x, axis=-1, keepdims=True)
            v = jnp.mean(jnp.square(x - m), axis=-1, keepdims=True)
            return (x - m) * jax.lax.rsqrt(v + LN_EPS) * w + b

        def _attention(q, k, v, scale):
            scores = jnp.einsum('bqd,bkd->bqk', q, k) * scale
            probs = jax.nn.softmax(scores, axis=-1)
            return jnp.einsum('bqk,bkd->bqd', probs, v)
        scale = EMBED_DIM ** (-0.5)
        norm_X = _layernorm(input_features, norm1_w, norm1_b)
        norm_F_L = _layernorm(query_feature, norm2_w, norm2_b)
        attended = _attention(norm_F_L, norm_X, norm_X, scale)
        h = jax.nn.gelu(attended @ fc1_w.T + fc1_b, approximate=False)
        cross_attended = h @ fc2_w.T + fc2_b
        norm_cross = _layernorm(cross_attended, norm3_w, norm3_b)
        self_attended = _attention(norm_cross, norm_cross, norm_cross, scale)
        skip_connect = cross_attended + gamma1 * self_attended
        return norm_F_L + gamma2 * skip_connect

    def _L2_xattn_ref(q, k, Wq, bq, Wk, bk, Wv, bv, W1, b1, W2, b2, ln_g, ln_b, use_causal_mask):
        import jax, jax.numpy as jnp
        import numpy as np
        B, S, D_MODEL, H, D_FF = (2, 512, 256, 16, 1024)
        D_HEAD = D_MODEL // H
        LN_EPS = 1e-05

        def _xavier(key, shape):
            fan_out, fan_in = shape
            std = (2.0 / (fan_in + fan_out)) ** 0.5
            return jax.random.normal(key, shape, dtype=jnp.float32) * std

        def _layer_norm(x, g, b):
            mu = jnp.mean(x, axis=-1, keepdims=True)
            var = jnp.mean((x - mu) ** 2, axis=-1, keepdims=True)
            return (x - mu) * jax.lax.rsqrt(var + LN_EPS) * g + b
        Bq, Sq, _ = q.shape
        Sk = k.shape[1]
        Q = q @ Wq.T + bq
        K = k @ Wk.T + bk
        V = k @ Wv.T + bv
        Q_ = Q.reshape(Bq, Sq, H, D_HEAD).transpose(0, 2, 1, 3)
        K_ = K.reshape(Bq, Sk, H, D_HEAD).transpose(0, 2, 1, 3)
        V_ = V.reshape(Bq, Sk, H, D_HEAD).transpose(0, 2, 1, 3)
        scores = jnp.einsum('bhqd,bhkd->bhqk', Q_, K_) / D_HEAD ** 0.5
        if use_causal_mask:
            causal = jnp.tril(jnp.ones((Sq, Sk), dtype=bool))
            scores = jnp.where(causal, scores, jnp.float32(-1000000000.0))
        sim = jax.nn.softmax(scores, axis=-1)
        att = jnp.einsum('bhqk,bhkd->bhqd', sim, V_)
        att_h = att.transpose(0, 2, 1, 3).reshape(Bq, Sq, D_MODEL)
        att_h = att_h + q
        att_h = _layer_norm(att_h, ln_g, ln_b)
        ff = jax.nn.gelu(att_h @ W1.T + b1, approximate=False) @ W2.T + b2
        return ff + att_h

    def _L3_xattn_ref(builder_state, base_state, input_ids, program_probs, A, Bmat, Cmat, W_in, b_in, W_qkv, b_qkv, W_o, b_o, W_prog, b_prog, g1, beta1, g2, beta2):
        import jax, jax.numpy as jnp
        import numpy as np
        BATCH, T, H, S, P, NH = (4, 512, 256, 64, 64, 8)
        HD = H // NH

        def _layernorm(x, g, b):
            mu = jnp.mean(x, axis=-1, keepdims=True)
            var = jnp.mean((x - mu) ** 2, axis=-1, keepdims=True)
            return (x - mu) * jax.lax.rsqrt(var + 1e-05) * g + b

        def _mha(q_in, kv_in, W_qkv, b_qkv, W_o, b_o):
            Wq, Wk, Wv = jnp.split(W_qkv, 3, axis=0)
            bq, bk, bv = jnp.split(b_qkv, 3, axis=0)

            def heads(x, W, b):
                y = x @ W.T + b
                return y.reshape(y.shape[0], y.shape[1], NH, HD).transpose(0, 2, 1, 3)
            q, k, v = (heads(q_in, Wq, bq), heads(kv_in, Wk, bk), heads(kv_in, Wv, bv))
            scores = jnp.einsum('bhqd,bhkd->bhqk', q, k) * (1.0 / np.sqrt(HD))
            attn = jax.nn.softmax(scores, axis=-1)
            out = jnp.einsum('bhqk,bhkd->bhqd', attn, v)
            out = out.transpose(0, 2, 1, 3).reshape(q_in.shape)
            return out @ W_o.T + b_o
        residual = builder_state
        x = _layernorm(builder_state, g1, beta1)
        base_n = _layernorm(base_state, g1, beta1)
        x = residual + _mha(x, base_n, W_qkv, b_qkv, W_o, b_o)
        residual = x
        xn = _layernorm(x, g2, beta2)
        U = (xn @ W_in.T + b_in) @ Bmat

        def step(s, u_t):
            s = jax.nn.silu(s @ A.T) + u_t
            return (s, s)
        _, states = jax.lax.scan(step, jnp.zeros((builder_state.shape[0], S), U.dtype), U.transpose(1, 0, 2))
        ssm_out = jnp.einsum('tbs,sh->bth', states, Cmat)
        x = residual + ssm_out
        mod = program_probs.mean(axis=1) @ W_prog.T + b_prog
        return x + mod[:, None, :]
    x = _L0_xattn_ref(x, ctx_1024, mask_BxSxS2_fk0, L0_xattn_Wq, L0_xattn_bq, L0_xattn_Wk, L0_xattn_bk, L0_xattn_Wv, L0_xattn_bv, L0_xattn_Wo, L0_xattn_bo, L0_xattn_Wg, L0_xattn_bg, L0_xattn_W1, L0_xattn_b1, L0_xattn_W2, L0_xattn_b2, L0_xattn_g1, L0_xattn_be1, L0_xattn_g2, L0_xattn_be2)
    x = _L1_xattn_ref(ctx_1024, x, L1_xattn_norm1_w, L1_xattn_norm1_b, L1_xattn_norm2_w, L1_xattn_norm2_b, L1_xattn_norm3_w, L1_xattn_norm3_b, L1_xattn_gamma1, L1_xattn_gamma2, L1_xattn_fc1_w, L1_xattn_fc1_b, L1_xattn_fc2_w, L1_xattn_fc2_b)
    x = _L2_xattn_ref(x, ctx_1024, L2_xattn_Wq, L2_xattn_bq, L2_xattn_Wk, L2_xattn_bk, L2_xattn_Wv, L2_xattn_bv, L2_xattn_W1, L2_xattn_b1, L2_xattn_W2, L2_xattn_b2, L2_xattn_ln_g, L2_xattn_ln_b, 1)
    x = _L3_xattn_ref(x, ctx_1024, itok_BxS2_4_31999, ctxb_2048x64, L3_xattn_A, L3_xattn_Bmat, L3_xattn_Cmat, L3_xattn_W_in, L3_xattn_b_in, L3_xattn_W_qkv, L3_xattn_b_qkv, L3_xattn_W_o, L3_xattn_b_o, L3_xattn_W_prog, L3_xattn_b_prog, L3_xattn_g1, L3_xattn_beta1, L3_xattn_g2, L3_xattn_beta2)
    return x

_drawn_inputs = setup_inputs


def setup_inputs(seed=0):
    import zlib

    import numpy as np

    out = dict(_drawn_inputs(seed))
    spreads = {'L0_xattn_bq': (0.0, 0.8),
     'L0_xattn_bk': (0.0, 0.8),
     'L0_xattn_bv': (0.0, 0.419),
     'L0_xattn_bo': (0.0, 0.1),
     'L0_xattn_bg': (0.0, 0.1),
     'L0_xattn_b1': (0.0, 0.354),
     'L0_xattn_b2': (0.0, 0.1),
     'L0_xattn_g1': (1.0, 0.6),
     'L0_xattn_be1': (0.0, 0.8),
     'L0_xattn_g2': (1.0, 0.6),
     'L0_xattn_be2': (0.0, 0.8),
     'L2_xattn_bq': (0.0, 0.563),
     'L2_xattn_bk': (0.0, 0.8),
     'L2_xattn_bv': (0.0, 0.1),
     'L2_xattn_b1': (0.0, 0.1),
     'L2_xattn_b2': (0.0, 0.1),
     'L2_xattn_ln_g': (1.0, 0.2),
     'L2_xattn_ln_b': (0.0, 0.1),
     'L3_xattn_b_in': (0.0, 0.1),
     'L3_xattn_b_qkv': (0.0, 0.1),
     'L3_xattn_b_o': (0.0, 0.1),
     'L3_xattn_b_prog': (0.0, 0.1),
     'L3_xattn_g1': (1.0, 0.2),
     'L3_xattn_beta1': (0.0, 0.1),
     'L3_xattn_g2': (1.0, 0.2),
     'L3_xattn_beta2': (0.0, 0.1)}
    factors = {'L0_xattn_Wq': 8.0, 'L0_xattn_Wk': 8.0, 'L1_xattn_fc1_b': 5.044}
    for name, (base, spread) in spreads.items():
        noise = np.random.default_rng([zlib.crc32(name.encode()), seed]).standard_normal(out[name].shape)
        drawn = base * np.exp(spread * noise) if base else spread * noise
        out[name] = jnp.asarray(drawn.astype(out[name].dtype))
    for name, factor in factors.items():
        out[name] = (out[name] * factor).astype(out[name].dtype)
    return out
```

```python
from contextlib import ExitStack

import concourse.bass as bass
from concourse import mybir

ALU = mybir.AluOpType
ACT = mybir.ActivationFunctionType
AX = mybir.AxisListType
F32 = mybir.dt.float32
BF16 = mybir.dt.bfloat16

P = 128
B = 16
D = 256
DC = D // P
FF = 1024
FC = FF // P
G = 4
NG = B // G
PAIR = 2
PT = PAIR * P
H16, H8 = 16, 8
SS = 64
PP = 64
EPS = 1e-5
NEG = -1e9

COLS = {}
_at = 0
for _name, _n in [("L0_g1", 2), ("L0_be1", 2), ("L0_bq", 2), ("L0_bk", 2), ("L0_bv", 2), ("L0_g2", 2), ("L0_be2", 2),
                  ("L0_b1", 8), ("L1_n1w", 2), ("L1_n1b", 2), ("L1_n2w", 2), ("L1_n2b", 2), ("L1_n3w", 2),
                  ("L1_n3b", 2), ("L2_bq", 2), ("L2_bk", 2), ("L2_bv", 2), ("L2_b1", 8), ("L2_g", 2), ("L2_b", 2),
                  ("L3_g1", 2), ("L3_be1", 2), ("L3_bq", 2), ("L3_bk", 2), ("L3_bv", 2), ("L3_g2", 2),
                  ("L3_be2", 2), ("L3_bin", 2)]:
    COLS[_name] = _at
    _at += _n
NCOL = _at
ROWS = {n: k for k, n in enumerate(["bo_bg", "bg", "L0_b2", "n2w", "n2b_all", "gamma2", "gamma1", "n3w", "n3b",
                                    "L2_g", "L2_b_b2", "L2_b2", "L3_bo", "b_prog"])}

QUADS = ([("L0", b, c) for b in range(G) for c in range(4)] + [("L1a", 0, 0)] + [("L1b", 0, 0)]
         + [("L2", b, c) for b in range(G) for c in range(4)] + [("L3", b, c) for b in range(G) for c in range(2)])
NQ = len(QUADS)
FIRST = {"L0": 0, "L1a": 16, "L1b": 17, "L2": 18, "L3": 34}
LAG_SUMS, LAG_TURN, LAG_MIX = 1, 3, 4


def attention(layer, n, insert):
    out = []
    for s in range(n + LAG_MIX):
        q = FIRST[layer] + s
        if s < n:
            out.append(("score", q))
        if 0 <= s - LAG_SUMS < n:
            out.append(("sums", q - LAG_SUMS))
        if 0 <= s - LAG_TURN < n:
            out.append(("turn", q - LAG_TURN))
        if 0 <= s - LAG_MIX < n:
            out.append(("mix", q - LAG_MIX))
        out += insert.get(s, [])
    assert all(s < n + LAG_MIX for s in insert)
    return out


def plan():
    def ln(key, p):
        return [("stat", key, p), ("norm", key, p)]

    def ffn1(layer, p):
        return [("ffn1", layer, p, k) for k in range(FC // 2)]

    s = ln("x", 0) + ln("x", 1)
    s += [("flip", "x", 0), ("q", "L0", 0), ("k", "L0", 0), ("v", "L0", 0)]
    s += [("flip", "x", 1), ("q", "L0", 1), ("k", "L0", 1), ("v", "L0", 1)]
    s += attention("L0", 16, {
        1: [("stat", "c", 0)], 2: [("norm", "c", 0)], 3: [("stat", "c", 1)], 4: [("norm", "c", 1)],
        5: [("flip", "c", 0)], 6: [("flip", "c", 1)], 7: [("flip", "cn", 0)], 8: [("flip", "cn", 1)],
        9: [("v", "L1", 0)],
        13: [("out", "L0", 0)], 14: [("stat", "x2", 0)], 15: [("norm", "x2", 0)], 16: [("flip", "x2", 0)],
        17: ffn1("L0", 0)[0:1], 18: ffn1("L0", 0)[1:2], 19: ffn1("L0", 0)[2:4]})
    s += [("out", "L0", 1), ("stat", "x2", 1), ("ffn2", "L0", 0), ("norm", "x2", 1), ("flip", "x2", 1)]
    s += [("stat", "x3", 0)] + ffn1("L0", 1)[0:2] + [("norm", "x3", 0)] + ffn1("L0", 1)[2:4]
    s += [("flip", "x3", 0), ("ffn2", "L0", 1), ("stat", "x3", 1), ("k", "L2", 0), ("norm", "x3", 1)]
    s += [("flip", "x3", 1)]
    s += [("score", 16), ("k", "L2", 1), ("sums", 16), ("v", "L2", 0), ("v", "L2", 1), ("turn", 16), ("k", "L3", 0),
          ("mix", 16), ("k", "L3", 1)]
    s += [("cross", "L1", 0), ("cross", "L1", 1)] + ln("cr", 0) + [("stat", "cr", 1), ("v", "L3", 0), ("norm", "cr", 1)]
    s += [("flip", "cr", 0), ("flip", "cr", 1), ("score", 17), ("v", "L3", 1), ("sums", 17), ("turn", 17)]
    s += [("self", "L1", 0), ("self", "L1", 1)]
    s += [("flip", "x4", 0), ("q", "L2", 0), ("flip", "x4", 1), ("q", "L2", 1)]
    s += attention("L2", 16, {
        13: [("flip", "o", 0)], 14: [("stat", "x5", 0)], 15: [("norm", "x5", 0)], 16: [("flip", "x5", 0)],
        17: ffn1("L2", 0)[0:1], 18: ffn1("L2", 0)[1:2], 19: ffn1("L2", 0)[2:4]})
    s += [("flip", "o", 1), ("stat", "x5", 1), ("ffn2", "L2", 0), ("norm", "x5", 1), ("flip", "x5", 1)]
    s += [("stat", "x6", 0)] + ffn1("L2", 1)[0:2] + [("norm", "x6", 0)] + ffn1("L2", 1)[2:4]
    s += [("flip", "x6", 0), ("q", "L3", 0), ("ffn2", "L2", 1), ("stat", "x6", 1), ("norm", "x6", 1)]
    s += [("flip", "x6", 1), ("q", "L3", 1)]
    s += attention("L3", 8, {8: [("out", "L3", 0)], 9: [("stat", "x7", 0)], 10: [("norm", "x7", 0)],
                             11: [("flip", "x7", 0)]})
    s += [("out", "L3", 1)] + ln("x7", 1) + [("flip", "x7", 1), ("drive", "L3", 0)]
    return s


STEPS = plan()
DENSE = [s for s in STEPS if s[0] in ("flip", "q", "k", "v", "out", "ffn1", "ffn2", "cross", "self", "drive")]
NB = 3
PAD = -len(DENSE) % NB
ND = (len(DENSE) + PAD) // NB
STATS = [s[1:] for s in STEPS if s[0] == "stat"]
NORMS = [s[1:] for s in STEPS if s[0] == "norm"]
MASKED = [s[1:] for s in STEPS if s[0] == "q"]
POOL_JOBS = ["xb", ("x2b", 0), ("x2b", 1), ("skip", 0), ("skip", 1), ("x5b", 0), ("x5b", 1),
             ("x6b", 0), ("x6b", 1), ("x7b", 0), ("x7b", 1)]
DVE_LINKS = 2 * len(STATS) + 3
POOL_LINKS = 6 + 2
O_USES = {("L0", b): b for b in range(G)} | {("L1a", 0): 4} | {("L2", b): 6 + b for b in range(G)} \
    | {("L3", b): 10 + b for b in range(G)}
NO = 14


def network(nc, a, out):
    with ExitStack() as ctx:
        def sb(name, shape, dt=F32):
            return ctx.enter_context(nc.sbuf_tensor(name, shape, dt))

        def bank(name):
            return ctx.enter_context(nc.psum_tensor(name, [P, 512], F32))

        def sem(name):
            return ctx.enter_context(nc.semaphore(name))

        def weight(name, k, n):
            return sb(name, [P, k, n])

        wq = {l: weight(f"{l}_wq", DC, D) for l in ("L0", "L2", "L3")}
        wk = {l: weight(f"{l}_wk", DC, D) for l in ("L0", "L2", "L3")}
        wv = {l: weight(f"{l}_wv", DC, D) for l in ("L0", "L2", "L3")}
        wo = {l: weight(f"{l}_wo", DC, D) for l in ("L0", "L3")}
        wg = weight("L0_wg", DC, D)
        w1 = {l: weight(f"{l}_w1", DC, FF) for l in ("L0", "L2")}
        w2 = {l: weight(f"{l}_w2", FC, D) for l in ("L0", "L2")}
        fc1 = weight("L1_fc1", DC, 4)
        fc2 = sb("L1_fc2", [5, D])
        w_drive = weight("w_drive", DC, SS)
        b_drive = sb("b_drive", [SS, 1])
        bmat = weight("bmat", DC, SS)
        a_t = sb("a_t", [SS, SS])
        w_last = sb("w_last", [P, D])
        cols = sb("cols", [P, NCOL])
        fc1_b = sb("fc1_b", [4, 1])
        rows = sb("rows", [P, len(ROWS), D])
        ident = sb("ident", [P, P])
        masks = sb("masks", [P, 4 + 4 + 2])
        causal = sb("causal", [P, P])
        half = sb("half", [P, 2])
        mean_w = sb("mean_w", [P, 1])

        x_in = sb("x_in", [P, G, D])
        c_in = sb("c_in", [P, G, D])
        cn = sb("cn", [P, G, D])
        bias = sb("bias", [P, G, P])
        cT = sb("cT", [P, DC, G * P])
        n1T = sb("n1T", [P, DC, G * P])
        n3T = sb("n3T", [P, DC, G * P])
        xn = sb("xn", [P, G, D])
        xn3 = sb("xn3", [P, G, D])
        cur = sb("cur", [P, G, D])
        res = sb("res", [P, G, D])
        cr = sb("cr", [P, G, D])
        actT = sb("actT", [P, DC, G * P])
        wide = sb("wide", [P, 2, 8 * PT])
        qm = wide[:].rearrange("p a (v c t) -> p a v c t", v=4, c=DC)
        hT = wide[:].rearrange("p a (k t) -> p a k t", k=FC)
        kT = sb("kT", [P, 2, DC, G * P])
        bk_half = sb("bk_half", [P, 2, 2, DC])
        k3T = sb("k3T", [P, DC, G * P])
        vpad = sb("vpad", [P, G, H16 // 2, 64])
        v3 = sb("v3", [P, G, D])
        v1 = sb("v1", [P, G, 4])
        oT = sb("oT", [P, DC, G * P])
        qs = oT[:].rearrange("p c t -> p (c t)").rearrange("p (a c t) -> p a c t", a=2, c=DC)
        h4 = sb("h4", [5, G * P])
        probs = sb("probs", [P, 4, 4, P])
        probsT = sb("probsT", [P, 2, 4, P])
        nmx = sb("nmx", [P, 4, 4])
        total = sb("total", [P, 4, 4])
        rtotal = sb("rtotal", [P, 4, 4])
        stats = sb("stats", [P, 2, 6])
        moments = sb("moments", [P, 2, 2, 2])
        veps = sb("veps", [P, 2, 2])
        rstd = sb("rstd", [P, 2, 2])
        x7_all = sb("x7_all", [P, B, D])
        u_all = sb("u_all", [SS, P, B])
        w_state = wide[0:SS, 0, :].rearrange("p (t b) -> p t b", b=B)
        stT = wide[:, 1, :].rearrange("p (b t) -> p b t", b=B)
        means = sb("means", [P, B])
        prog = wide[:, 1, 0:B * PP].rearrange("p (b s) -> p b s", b=B)
        w_in = wide[:, 0, 0:DC * D].rearrange("p (k n) -> p k n", k=DC)
        y_out = probs[:].rearrange("p a b c -> p (a b c)").rearrange("p (n d) -> p n d", d=D)

        s_bank = [bank(f"s_bank{i}") for i in range(2)]
        t_bank = [bank(f"t_bank{i}") for i in range(2)]
        o_bank = bank("o_bank")
        d_bank = [bank(f"d_bank{i}") for i in range(NB)]

        first_loaded, rows_loaded = sem("first_loaded"), sem("rows_loaded")
        l0_loaded, rest_loaded = sem("l0_loaded"), sem("rest_loaded")
        prog_loaded, prog_meant = sem("prog_loaded"), sem("prog_meant")
        x_loaded, c_loaded = sem("x_loaded"), sem("c_loaded")
        out_stored = sem("out_stored")
        set_up = sem("set_up")
        set_up_dve = sem("set_up_dve")
        set_up_pe = sem("set_up_pe")
        bias_ready = sem("bias_ready")
        scored = sem("scored")
        maxed = sem("maxed")
        exped = sem("exped")
        rsummed = sem("rsummed")
        weighed = sem("weighed")
        turned = sem("turned")
        copied = sem("copied")
        mixed = sem("mixed")
        o_copied = sem("o_copied")
        filled = [sem(f"filled{i}") for i in range(NB)]
        drained = [sem(f"drained{i}") for i in range(NB)]
        masked = sem("masked")
        var_ready = sem("var_ready")
        rstd_ready = sem("rstd_ready")
        normed = sem("normed")
        summed = sem("summed")
        dve_waited = sem("dve_waited")
        dve_link, pool_link = sem("dve_link"), sem("pool_link")
        prefilled, stepped, silued = sem("prefilled"), sem("stepped"), sem("silued")
        states_ready, means_ready, last_filled = sem("states_ready"), sem("means_ready"), sem("last_filled")
        last_added = sem("last_added")

        LEAD = {"quads": 2, "turned": 4, "copied": 2, "mixed": 2, "o": 1, "dense": 1}

        def quads_done(i, n):
            return i * NQ + n + 1

        def dense_slot(step):
            n = DENSE.index(step)
            return n % NB, n // NB

        def drained_at(i, *step):
            slot, n = dense_slot(step)
            return drained[slot], i * ND + n + 1 + LEAD["dense"]

        def normed_at(i, *key):
            return normed, i * len(NORMS) + NORMS.index(key) + 1

        def summed_at(i, job):
            return summed, i * len(POOL_JOBS) + POOL_JOBS.index(job) + 1

        def o_used(i, n):
            return i * NO + n

        def pair(t, p):
            return t[:, PAIR * p:PAIR * p + PAIR, :]

        def toks(t, c, p):
            return t[:, c, PT * p:PT * p + PT]

        def row(name):
            return rows[:, ROWS[name], :]

        def rows_over(name, n):
            return rows[:, ROWS[name]:ROWS[name] + 1, :].broadcast_to([P, n, D])

        def col(name, c):
            return cols[:, COLS[name] + c:COLS[name] + c + 1]

        block = ctx.enter_context(nc.Block())
        FIRST_LOADS = [(ident[:], a["ident"]), (cols[:], a["cols"]), (masks[:], a["masks"]),
                       (wq["L0"][:], a["L0_wq"]), (wk["L0"][:], a["L0_wk"]), (wv["L0"][:], a["L0_wv"]),
                       (w_in, a["L3_w_in"]), (bmat[:], a["L3_bmat"]), (causal[:], a["causal"]),
                       (fc1[:], a["L1_fc1"]), (fc1_b[:], a["fc1_b"]), (a_t[:], a["a_t"])]
        L0_LOADS = [(wo["L0"][:], a["L0_wo"]), (wg[:], a["L0_wg"]), (w1["L0"][:], a["L0_w1"]), (w2["L0"][:], a["L0_w2"])]
        REST_LOADS = [(wk["L2"][:], a["L2_wk"]), (wv["L2"][:], a["L2_wv"]), (wk["L3"][:], a["L3_wk"]),
                      (wv["L3"][:], a["L3_wv"]), (fc2[0:4, :], a["fc2"]), (fc2[4:5, :], a["fc2_b"]),
                      (wq["L2"][:], a["L2_wq"]), (w1["L2"][:], a["L2_w1"]), (w2["L2"][:], a["L2_w2"]),
                      (wq["L3"][:], a["L3_wq"]), (wo["L3"][:], a["L3_wo"]), (w_last[0:SS, :], a["cmat"]),
                      (w_last[SS:P, :], a["wprog"])]

        @block.sync
        def _(sp):
            def load_x(i):
                sp.dma_start(x_in[:], a["x"][bass.ds(i * G, G)].rearrange("b s d -> s b d")).then_inc(x_loaded, 16)

            def load_c(i):
                sp.dma_start(c_in[:], a["ctx"][bass.ds(i * G, G)].rearrange("b s d -> s b d")).then_inc(c_loaded, 16)
                sp.dma_start(bias[:], a["mask"][bass.ds(i * G, G)].rearrange("b q k -> q b k")).then_inc(c_loaded, 16)

            load_x(0)
            for t, name in FIRST_LOADS[:7]:
                sp.dma_start(t, name).then_inc(first_loaded, 16)
            load_c(0)
            for t, name in FIRST_LOADS[7:]:
                sp.dma_start(t, name).then_inc(first_loaded, 16)
            sp.dma_start(rows[:].rearrange("p r d -> p (r d)"), a["rows"].broadcast_to([P, len(ROWS) * D]))\
                .then_inc(rows_loaded, 16)
            for t, name in L0_LOADS:
                sp.dma_start(t, name).then_inc(l0_loaded, 16)
            for t, name in REST_LOADS:
                sp.dma_start(t, name).then_inc(rest_loaded, 16)
            with sp.Fori(1, NG) as i:
                sp.wait_ge(*summed_at(i - 1, "xb"))
                sp.wait_ge(*normed_at(i - 1, "x", 1))
                load_x(i)
                sp.wait_ge(*normed_at(i - 1, "c", 1))
                sp.wait_ge(*drained_at(i - 1, "flip", "c", 1))
                sp.wait_ge(maxed, quads_done(i - 1, 15) + LEAD["quads"])
                load_c(i)
            sp.wait_ge(*drained_at(NG - 1, "drive", "L3", 0))
            sp.dma_start(prog, a["prog"].rearrange("b s k -> s b k")).then_inc(prog_loaded, 16)
            with sp.Fori(0, B // 8) as j:
                sp.wait_ge(last_added, j * 4 + 4)
                sp.dma_start(out[bass.ds(j * 8, 8)].rearrange("b s d -> s b d"),
                             x7_all[:, bass.ds(j * 8, 8), :]).then_inc(out_stored, 16)
            sp.wait_ge(out_stored, 16 * (B // 8))

        def score_operands(q, j):
            layer, b, c = QUADS[q]
            p, t = b // PAIR, (b % PAIR) * P
            if layer in ("L0", "L2"):
                return [(qm[:, p, j, c // 2, t:t + P], kT[:, c % 2, c // 2, b * P:b * P + P])]
            if layer == "L3":
                return [(qm[:, p, j, c, t:t + P], k3T[:, c, b * P:b * P + P])]
            keysT = n1T if layer == "L1a" else actT
            return [(actT[:, k, j * P:j * P + P], keysT[:, k, j * P:j * P + P]) for k in range(DC)]

        BIASED = ("L0", "L2")

        @block.tensor
        def _(pe):
            def wait_drained(i, needs, own=None):
                want = {}
                if own is not None:
                    slot, n = dense_slot(own)
                    want[slot] = n
                for need in needs:
                    slot, n = dense_slot(need)
                    want[slot] = max(want.get(slot, 0), n + 1)
                for slot, n in want.items():
                    pe.wait_ge(drained[slot], i * ND + n + LEAD["dense"])

            def dense(i, step, *needs):
                wait_drained(i, needs, step)
                slot, _ = dense_slot(step)
                return d_bank[slot], filled[slot]

            def flip(i, key, p):
                src = {"x": xn, "x2": xn, "x6": xn, "x7": xn, "x3": xn3, "x5": xn3, "c": c_in, "cn": cn, "cr": cn,
                       "x4": cur}.get(key)
                needs = []
                if key == "c":
                    pe.wait_ge(c_loaded, i * 32 + 32)
                elif key == "x4":
                    needs = [("self", "L1", p)]
                elif key == "o":
                    pe.wait_ge(o_copied, o_used(i, O_USES["L2", 2 * p + 1] + 1) + LEAD["o"])
                elif key == "cn":
                    pe.wait_ge(*normed_at(i, "c", p))
                else:
                    pe.wait_ge(*normed_at(i, key, p))
                d, done = dense(i, ("flip", key, p), *needs)
                for b in range(PAIR):
                    for c in range(DC):
                        if key == "o":
                            mm = nc.tensor.transpose(d[:, b * D + c * P:b * D + c * P + P],
                                                     oT[:, c, PT * p + b * P:PT * p + b * P + P], ident[:])
                        else:
                            mm = nc.tensor.transpose(d[:, c * PT + b * P:c * PT + b * P + P],
                                                     src[:, PAIR * p + b, c * P:c * P + P], ident[:])
                mm.then_inc(done, 1)

            def project(i, step, w, xT, p, *needs):
                d, done = dense(i, step, *needs)
                for m in range(DC):
                    for k in range(DC):
                        mm = nc.tensor.matmul(d[:, m * PT:m * PT + PT], w[:, k, m * P:m * P + P], toks(xT, k, p),
                                              start=(k == 0), stop=(k == DC - 1))
                mm.then_inc(done, 1)

            def project_rows(i, step, terms, p, *needs):
                d, done = dense(i, step, *needs)
                for b in range(PAIR):
                    todo = [(xT, w, k) for xT, w, chunks in terms for k in range(chunks)]
                    for n, (xT, w, k) in enumerate(todo):
                        mm = nc.tensor.matmul(d[:, b * D:b * D + D], xT(k, b), w[:, k, :],
                                              start=(n == 0), stop=(n == len(todo) - 1))
                mm.then_inc(done, 1)

            def of(t, p):
                return lambda k, b: t[:, k, PT * p + b * P:PT * p + b * P + P]

            pe.wait_ge(first_loaded, 16 * len(FIRST_LOADS))
            for m in range(DC):
                for k in range(DC):
                    nc.tensor.matmul(o_bank[:, m * SS:m * SS + SS], w_in[:, k, m * P:m * P + P], bmat[:, k, :],
                                     start=(k == 0), stop=(k == DC - 1))
            for k in range(DC):
                mm = nc.tensor.matmul(o_bank[0:SS, 128:129], bmat[:, k, :], col("L3_bin", k),
                                 start=(k == 0), stop=(k == DC - 1))
            mm.then_inc(set_up_pe, 1)
            pe.wait_ge(set_up_dve, 2)

            def turn(i):
                for step in STEPS:
                    kind, key = step[0], step[1]
                    p = step[2] if len(step) > 2 else 0
                    if kind == "flip":
                        flip(i, key, p)
                    elif kind == "q":
                        project(i, step, wq[key], actT, p, ("flip", {"L0": "x", "L2": "x4", "L3": "x6"}[key], p))
                    elif kind == "k":
                        if key == "L2":
                            pe.wait_ge(rest_loaded, 16 * len(REST_LOADS))
                        project(i, step, wk[key], {"L0": actT, "L2": cT, "L3": n3T}[key], p,
                                ("flip", {"L0": "x", "L2": "c", "L3": "cn"}[key], p))
                    elif kind == "v" and key == "L1":
                        d, done = dense(i, step, ("flip", "cn", 0), ("flip", "cn", 1))
                        for b in range(G):
                            for k in range(DC):
                                mm = nc.tensor.matmul(d[:, 4 * b:4 * b + 4], n1T[:, k, b * P:b * P + P], fc1[:, k, :],
                                                      start=(k == 0), stop=(k == DC - 1))
                        mm.then_inc(done, 1)
                    elif kind == "v":
                        xT = {"L0": actT, "L2": cT, "L3": n3T}[key]
                        project_rows(i, step, [(of(xT, p), wv[key], DC)], p,
                                     ("flip", {"L0": "x", "L2": "c", "L3": "cn"}[key], p))
                    elif kind == "score":
                        scores(i, key)
                    elif kind == "turn":
                        pe.wait_ge(weighed, quads_done(i, key))
                        pe.wait_ge(copied, quads_done(i, key) - 2 + LEAD["copied"])
                        for j in range(4):
                            mm = nc.tensor.transpose(t_bank[key % 2][:, j * P:j * P + P], probs[:, key % 4, j, :],
                                                     ident[:])
                        mm.then_inc(turned, 1)
                    elif kind == "mix":
                        mix(i, key)
                    elif kind == "out":
                        n = O_USES[key, 2 * p + 1] + 1
                        pe.wait_ge(o_copied, o_used(i, n) + LEAD["o"])
                        terms = [(of(oT, p), wo[key], DC)]
                        if key == "L0":
                            pe.wait_ge(l0_loaded, 16 * len(L0_LOADS))
                            terms.append((of(cT, p), wg, DC))
                        project_rows(i, step, terms, p, *([("flip", "c", p)] if key == "L0" else []))
                    elif kind == "ffn1":
                        k0 = 2 * step[3]
                        d, done = dense(i, step, ("flip", {"L0": "x2", "L2": "x5"}[key], p))
                        for m in range(2):
                            for k in range(DC):
                                mm = nc.tensor.matmul(d[:, m * PT:m * PT + PT],
                                                      w1[key][:, k, (k0 + m) * P:(k0 + m) * P + P], toks(actT, k, p),
                                                      start=(k == 0), stop=(k == DC - 1))
                        mm.then_inc(done, 1)
                    elif kind == "ffn2":
                        project_rows(i, step, [(lambda k, b: hT[:, p, k, b * P:b * P + P], w2[key], FC)], p,
                                     *[("ffn1", key, p, k) for k in range(FC // 2)])
                    elif kind == "cross":
                        pe.wait_ge(o_copied, o_used(i, O_USES["L1a", 0] + 2) + LEAD["o"])
                        d, done = dense(i, step)
                        for b in range(PAIR):
                            t = PT * p + b * P
                            mm = nc.tensor.matmul(d[:, b * D:b * D + D], h4[:, t:t + P], fc2[:], start=True, stop=True)
                        mm.then_inc(done, 1)
                    elif kind == "self":
                        pe.wait_ge(copied, quads_done(i, FIRST["L1b"]) + LEAD["copied"])
                        d, done = dense(i, step)
                        for b in range(PAIR):
                            mm = nc.tensor.matmul(d[:, b * D:b * D + D],
                                                  probsT[:, FIRST["L1b"] % 2, PAIR * p + b, :],
                                                  cn[:, PAIR * p + b, :], start=True, stop=True)
                        mm.then_inc(done, 1)
                        if p == 1:
                            pe.wait_ge(done, i * ND + dense_slot(step)[1] + 1)
                            pe.sem_inc(mixed, 1)
                    elif kind == "drive":
                        d, done = dense(i, step, ("flip", "x7", 0), ("flip", "x7", 1))
                        for k in range(DC):
                            mm = nc.tensor.matmul(d[0:SS, :], w_drive[:, k, :], actT[:, k, :],
                                                  start=(k == 0), stop=(k == DC - 1))
                        mm.then_inc(done, 1)
                for n in range(len(DENSE), len(DENSE) + PAD):
                    pe.wait_ge(drained[n % NB], i * ND + n // NB + LEAD["dense"])
                    pe.sem_inc(filled[n % NB], 1)

            def scores(i, q):
                layer, b, c = QUADS[q]
                last = QUADS[(q - 2) % NQ][0]
                pe.wait_ge(maxed if last in BIASED else exped, quads_done(i, q) - 2 + LEAD["quads"])
                if layer in ("L0", "L2", "L3"):
                    wait_drained(i, [("k", layer, b // PAIR)])
                    pe.wait_ge(masked, i * len(MASKED) + MASKED.index((layer, b // PAIR)) + 1)
                else:
                    wait_drained(i, [("flip", {"L1a": "x3", "L1b": "cr"}[layer], p) for p in range(2)])
                for j in range(4):
                    ops = score_operands(q, j)
                    for n, (queries, keys) in enumerate(ops):
                        mm = nc.tensor.matmul(s_bank[q % 2][:, j * P:j * P + P], queries, keys,
                                              start=(n == 0), stop=(n == len(ops) - 1))
                mm.then_inc(scored, 1)

            def mix(i, q):
                layer, b, c = QUADS[q]
                pe.wait_ge(copied, quads_done(i, q) + LEAD["copied"])
                pT = probsT[:, q % 2]
                if layer == "L1a":
                    pe.wait_ge(o_copied, o_used(i, O_USES["L1a", 0]) + LEAD["o"])
                    pe.wait_ge(*drained_at(i, "v", "L1", 0))
                    for j in range(4):
                        mm = nc.tensor.matmul(o_bank[0:4, j * P:j * P + P], v1[:, j, :], pT[:, j, :],
                                              start=True, stop=True)
                    mm.then_inc(mixed, 1)
                    return
                n = O_USES[layer, b]
                at = 0
                if c == 0:
                    pe.wait_ge(*drained_at(i, "v", layer, b // PAIR))
                    pe.wait_ge(o_copied, o_used(i, n) + LEAD["o"])
                if layer == "L3":
                    for j in range(4):
                        mm = nc.tensor.matmul(o_bank[32 * j:32 * j + 32, at + c * P:at + c * P + P],
                                              v3[:, b, (4 * c + j) * 32:(4 * c + j) * 32 + 32], pT[:, j, :],
                                              start=True, stop=True)
                else:
                    for j in range(4):
                        h = 4 * c + j
                        lo = 32 * ((h % 8) // 2)
                        mm = nc.tensor.matmul(o_bank[lo:lo + 32, at + (c // 2) * P:at + (c // 2) * P + P],
                                              vpad[:, b, h // 2, 32 * (h % 2):32 * (h % 2) + 32], pT[:, j, :],
                                              start=(j % 2 == 0), stop=(j % 2 == 1))
                mm.then_inc(mixed, 1)

            with pe.Fori(0, NG) as i:
                turn(i)

            z = [s_bank[0], s_bank[1], t_bank[0], t_bank[1]]
            pe.wait_ge(*drained_at(NG - 1, "drive", "L3", 0))
            pe.wait_ge(copied, quads_done(NG - 1, NQ - 1) + LEAD["copied"])
            for n in range(4):
                lo = 32 * n - 1 if n else 0
                dst = z[n][0:SS, 0:512] if n else z[n][0:SS, B:512]
                mm = nc.tensor.matmul(dst, a_t[:], u_all[:, lo:32 * n + 31, :], start=True, stop=(n == 0),
                                      skip_group_check=True)
            for t in range(1, P):
                if t == 2:
                    pe.wait_ge(prog_loaded, 16)
                    for b in range(B):
                        means_mm = nc.tensor.matmul(o_bank[SS:P, b:b + 1], prog[:, b, :], mean_w[:], start=True,
                                                    stop=True)
                    means_mm.then_inc(prog_meant, 1)
                if t > 1:
                    pe.wait_ge(silued, t - 1)
                    mm = nc.tensor.matmul(z[t // 32][0:SS, (t % 32) * B:(t % 32) * B + B], a_t[:],
                                          w_state[:, t - 1, :], start=False, stop=True, skip_group_check=True)
                mm.then_inc(stepped, 1)

            pe.wait_ge(means_ready, 2)
            for n in range(B // PAIR):
                pe.wait_ge(states_ready, n // 2 + 1)
                if n >= NB:
                    pe.wait_ge(last_added, n - NB + 1)
                for b in range(PAIR):
                    mm = nc.tensor.matmul(d_bank[n % NB][:, b * D:b * D + D], stT[:, PAIR * n + b, :], w_last[:],
                                          start=True, stop=True)
                mm.then_inc(last_filled, 1)

        @block.gpsimd
        def _(pool):
            linked = [0]

            def link(ins, i=None):
                linked[0] += 1
                ins.then_inc(pool_link, 1)
                pool.wait_ge(pool_link, linked[0] if i is None else i * POOL_LINKS + base + linked[0] - base)

            nc.gpsimd.memset(half[:], -0.5)
            nc.gpsimd.memset(mean_w[:], 1.0 / P).then_inc(set_up, 1)
            nc.gpsimd.memset(h4[:], 1.0).then_inc(set_up, 1)
            nc.gpsimd.memset(vpad[:], 0.0).then_inc(set_up, 1)
            for s, lead in [(maxed, LEAD["quads"]), (exped, LEAD["quads"]), (turned, LEAD["turned"]),
                            (copied, LEAD["copied"]), (mixed, LEAD["mixed"]), (o_copied, LEAD["o"])] \
                    + [(s, LEAD["dense"]) for s in drained]:
                pool.sem_inc(s, lead)
            pool.wait_ge(rows_loaded, 16)
            nc.gpsimd.tensor_tensor(row("bo_bg"), row("bo_bg"), row("bg"), ALU.add)
            nc.gpsimd.tensor_tensor(row("L2_b_b2"), row("L2_b_b2"), row("L2_b2"), ALU.add)
            link(nc.gpsimd.tensor_tensor(row("gamma1"), row("gamma1"), row("gamma2"), ALU.mult))
            nc.gpsimd.tensor_tensor(row("n3w"), row("n3w"), row("gamma1"), ALU.mult)
            link(nc.gpsimd.tensor_tensor(row("n3b"), row("n3b"), row("gamma1"), ALU.mult))
            link(nc.gpsimd.tensor_tensor(row("n2b_all"), row("n2b_all"), row("n3b"), ALU.add))
            base = linked[0]

            def turn(i):
                linked[0] = base

                def job(i, name, ins):
                    ins.then_inc(summed, 1)

                def add(out, a0, a1, op=ALU.add):
                    return nc.gpsimd.tensor_tensor(out, a0, a1, op)

                for step in STEPS:
                    kind, key = step[0], step[1]
                    if kind == "stat":
                        n = STATS.index(step[1:])
                        pool.wait_ge(var_ready, i * len(STATS) + n + 1)
                        add(rstd[:, n % 2, :], veps[:, n % 2, :], half[:], ALU.pow).then_inc(rstd_ready, 1)
                    if kind == "sums":
                        pool.wait_ge(rsummed, quads_done(i, key))
                        r = rtotal[:, key % 4, :].unsqueeze(2).broadcast_to([P, 4, P])
                        add(probs[:, key % 4], probs[:, key % 4], r, ALU.mult).then_inc(weighed, 1)
                    if kind == "stat" and step[1:] == ("c", 0):
                        pool.wait_ge(x_loaded, i * 16 + 16)
                        job(i, "xb", add(res[:], x_in[:], rows_over("bo_bg", G)))
                    if kind == "norm" and key in ("x2", "x3", "x5", "x6", "x7"):
                        p = step[2]
                        c2, r2 = pair(cur, p), pair(res, p)
                        pool.wait_ge(*normed_at(i, key, p))
                        if key == "x2":
                            job(i, ("x2b", p), add(r2, c2, rows_over("L0_b2", PAIR)))
                        if key == "x3":
                            link(add(r2, pair(xn3, p), rows_over("n2w", PAIR), ALU.mult), i)
                            link(add(r2, r2, rows_over("n2b_all", PAIR)), i)
                        if key == "x5":
                            link(add(r2, pair(xn3, p), rows_over("L2_g", PAIR), ALU.mult), i)
                            job(i, ("x5b", p), add(r2, r2, rows_over("L2_b_b2", PAIR)))
                        if key == "x6":
                            job(i, ("x6b", p), add(r2, c2, rows_over("L3_bo", PAIR)))
                        if key == "x7":
                            x7 = x7_all[:, bass.ds(i * G + PAIR * p, PAIR), :]
                            job(i, ("x7b", p), add(x7, c2, rows_over("b_prog", PAIR)))
                    if kind == "norm" and key == "cr":
                        p = step[2]
                        c2, r2 = pair(cr, p), pair(res, p)
                        pool.wait_ge(*normed_at(i, key, p))
                        link(add(c2, c2, rows_over("gamma2", PAIR), ALU.mult), i)
                        job(i, ("skip", p), add(r2, r2, c2))
                assert linked[0] == base + POOL_LINKS, linked[0] - base

            with pool.Fori(0, NG) as i:
                turn(i)
            for g in range(4):
                pool.wait_ge(silued, P - 1)
                w = w_state[:, :, 4 * g:4 * g + 4].rearrange("p t b -> p b t")
                u = u_all[:, :, 4 * g:4 * g + 4].rearrange("p t b -> p b t")
                nc.gpsimd.tensor_tensor(stT[0:SS, 4 * g:4 * g + 4, :], w, u, ALU.add).then_inc(states_ready, 1)

        @block.vector
        def _(dve):
            linked = [0]
            base = [0]

            def link(ins, i=None):
                linked[0] += 1
                ins.then_inc(dve_link, 1)
                dve.wait_ge(dve_link, linked[0] if i is None else i * DVE_LINKS + linked[0])

            def dense_ready(i, *step):
                slot, n = dense_slot(step)
                dve.wait_ge(filled[slot], i * ND + n + 1)
                return d_bank[slot], drained[slot]

            dve.wait_ge(first_loaded, 16 * len(FIRST_LOADS))
            for name, by in (("L1_n2w", D ** -0.5), ("L1_n3w", D ** -0.25)):
                both = cols[:, COLS[name]:COLS[name] + 2 * DC]
                nc.vector.tensor_scalar(both, both, by, None, ALU.mult)
            for l, name in enumerate(("L0_bk", "L2_bk")):
                for h in range(2):
                    ins = nc.vector.tensor_scalar(bk_half[:, l, h, :], cols[:, COLS[name]:COLS[name] + DC],
                                                  masks[:, 8 + h:9 + h], None, ALU.mult)
            ins.then_inc(set_up_dve, 1)
            dve.wait_ge(set_up_pe, 1)
            nc.vector.tensor_copy(w_drive[:], o_bank[:, 0:DC * SS].rearrange("p (m s) -> p m s", m=DC))
            nc.vector.tensor_copy(b_drive[:], o_bank[0:SS, 128:129]).then_inc(set_up_dve, 1)

            def stat(i, key, p, n):
                src, ready = {"x": (x_in, None), "c": (c_in, None), "x2": (cur, ("out", "L0", p)),
                              "x3": (cur, ("ffn2", "L0", p)), "cr": (cr, ("cross", "L1", p)),
                              "x5": (cur, ("flip", "o", p)), "x6": (cur, ("ffn2", "L2", p)),
                              "x7": (cur, ("out", "L3", p))}[key]
                if key == "x":
                    dve.wait_ge(x_loaded, i * 16 + 16)
                elif key == "c":
                    dve.wait_ge(c_loaded, i * 32 + 32)
                else:
                    dve.wait_ge(*drained_at(i, *ready))
                for b in range(PAIR):
                    ins = nc.vector.bn_stats(stats[:, b, :], src[:, PAIR * p + b, :])
                link(ins, i)
                dve.sem_inc(dve_waited, 1)
                for b in range(PAIR):
                    ins = nc.vector.bn_aggr(moments[:, n % 2, b, :], stats[:, b, :])
                link(ins, i)
                nc.vector.tensor_scalar(veps[:, n % 2, :], moments[:, n % 2, :, 1], EPS, None, ALU.add)\
                    .then_inc(var_ready, 1)

            def norm(i, key, p, n):
                src, dst = {"x": (x_in, xn), "c": (c_in, cn), "x2": (cur, xn), "x3": (cur, xn3), "cr": (cr, cn),
                            "x5": (cur, xn3), "x6": (cur, xn), "x7": (cur, xn)}[key]
                dve.wait_ge(rstd_ready, i * len(STATS) + n + 1)
                for b in range(PAIR):
                    ins = nc.vector.tensor_scalar(dst[:, PAIR * p + b, :], src[:, PAIR * p + b, :],
                                                  moments[:, n % 2, b, 0:1], rstd[:, n % 2, b:b + 1],
                                                  ALU.subtract, ALU.mult)
                ins.then_inc(normed, 1)

            def affine(dst, d, p, g, b, done):
                for c in range(DC):
                    ins = nc.vector.tensor_scalar(toks(dst, c, p), d[:, c * PT:c * PT + PT], col(g, c), col(b, c),
                                                  ALU.mult, ALU.add)
                if done is not None:
                    ins.then_inc(done, 1)

            def turn(i):
                linked[0] = 0
                dve.wait_ge(c_loaded, i * 32 + 32)
                link(nc.vector.tensor_scalar(bias[:], bias[:], 1.0, -NEG, ALU.subtract, ALU.mult), i)
                for step in STEPS:
                    kind, key = step[0], step[1]
                    p = step[2] if len(step) > 2 else 0
                    if kind == "stat":
                        stat(i, key, p, STATS.index((key, p)))
                    elif kind == "norm":
                        norm(i, key, p, STATS.index((key, p)))
                    elif kind == "flip" and key in ("x", "x2", "x3", "cr", "x5", "x6", "x7"):
                        d, done = dense_ready(i, *step)
                        g, b = {"x": ("L0_g1", "L0_be1"), "x2": ("L0_g2", "L0_be2"), "x3": ("L1_n2w", "L1_n2b"),
                                "cr": ("L1_n3w", "L1_n3b"), "x5": ("L2_g", "L2_b"), "x6": ("L3_g1", "L3_be1"),
                                "x7": ("L3_g2", "L3_be2")}[key]
                        affine(actT, d, p, g, b, done)
                    elif kind == "flip" and key == "o":
                        d, done = dense_ready(i, *step)
                        nc.vector.tensor_tensor(pair(cur, p), d[:].rearrange("p (b n) -> p b n", b=PAIR), pair(cur, p),
                                                ALU.add).then_inc(done, 1)
                    elif kind == "q":
                        dve.wait_ge(*drained_at(i, *step))
                        m0 = 4 if key == "L3" else 0
                        for v in range(4):
                            ins = nc.vector.tensor_scalar(qm[:, p, v], qs[:, p], masks[:, m0 + v:m0 + v + 1], None,
                                                          ALU.mult)
                        ins.then_inc(masked, 1)
                    elif kind == "v" and key in ("L0", "L2"):
                        d, done = dense_ready(i, *step)
                        heads = d[:].rearrange("p (b h e n) -> p b h e n", b=PAIR, h=H16 // 2, e=2)
                        for e, lo in ((0, 0), (1, 48)):
                            for b in range(PAIR):
                                ins = nc.vector.tensor_copy(vpad[:, PAIR * p + b, :, lo:lo + 16], heads[:, b, :, e, :])
                        ins.then_inc(done, 1)
                    elif kind == "score":
                        maximum(i, key)
                    elif kind == "sums":
                        dve.wait_ge(exped, quads_done(i, key) + LEAD["quads"])
                        nc.vector.reciprocal(rtotal[:, key % 4, :], total[:, key % 4, :]).then_inc(rsummed, 1)
                    elif kind == "turn":
                        dve.wait_ge(turned, quads_done(i, key) + LEAD["turned"])
                        dve.wait_ge(mixed, quads_done(i, key) - 2 + LEAD["mixed"])
                        nc.vector.tensor_copy(probsT[:, key % 2].rearrange("p j k -> p (j k)"), t_bank[key % 2][:])\
                            .then_inc(copied, 1)
                    elif kind == "mix" and QUADS[key][0] in ("L0", "L2", "L3"):
                        layer, b, c = QUADS[key]
                        if c == {"L0": 3, "L2": 3, "L3": 1}[layer]:
                            dve.wait_ge(mixed, quads_done(i, key) + LEAD["mixed"])
                            at = 0
                            name = COLS[f"{layer}_bv"]
                            bv = cols[:, name:name + DC].unsqueeze(2).broadcast_to([P, DC, P])
                            nc.vector.tensor_tensor(oT[:, :, b * P:b * P + P],
                                                    o_bank[:, at:at + 256].rearrange("p (c t) -> p c t", c=DC), bv,
                                                    ALU.add).then_inc(o_copied, 1)
                    elif kind in ("out", "ffn2"):
                        d, done = dense_ready(i, *step)
                        name = {("out", "L0"): "xb", ("ffn2", "L0"): ("x2b", p), ("ffn2", "L2"): ("x5b", p),
                                ("out", "L3"): ("x6b", p)}[kind, key]
                        dve.wait_ge(*summed_at(i, name))
                        nc.vector.tensor_tensor(pair(cur, p), d[:].rearrange("p (b n) -> p b n", b=PAIR), pair(res, p),
                                                ALU.add).then_inc(done, 1)
                    elif kind == "ffn1" and key == "L0":
                        d, done = dense_ready(i, *step)
                        for m in range(2):
                            k = 2 * step[3] + m
                            ins = nc.vector.tensor_scalar(hT[:, p, k, :], d[:, m * PT:m * PT + PT], col("L0_b1", k),
                                                          0.0, ALU.add, ALU.max)
                        ins.then_inc(done, 1)
                    elif kind == "self":
                        d, done = dense_ready(i, *step)
                        link(nc.vector.tensor_tensor(pair(cur, p), d[:].rearrange("p (b n) -> p b n", b=PAIR),
                                                     rows_over("n3w", PAIR), ALU.mult), i)
                        dve.wait_ge(*summed_at(i, ("skip", p)))
                        nc.vector.tensor_tensor(pair(cur, p), pair(cur, p), pair(res, p), ALU.add).then_inc(done, 1)
                    elif kind == "drive":
                        d, done = dense_ready(i, *step)
                        nc.vector.tensor_scalar(u_all[:, :, bass.ds(i * G, G)],
                                                d[0:SS, :].rearrange("p (b t) -> p t b", b=G), b_drive[:], None,
                                                ALU.add).then_inc(done, 1)
                for n in range(len(DENSE), len(DENSE) + PAD):
                    dve.wait_ge(filled[n % NB], i * ND + n // NB + 1)
                    dve.sem_inc(drained[n % NB], 1)
                assert linked[0] == DVE_LINKS, linked[0]

            def maximum(i, q):
                layer, b, c = QUADS[q]
                dve.wait_ge(scored, quads_done(i, q))
                dve.wait_ge(turned, quads_done(i, q) - 4 + LEAD["turned"])
                if layer in BIASED:
                    dve.sem_inc(dve_waited, 1)
                    for j in range(4):
                        more = bias[:, b, :] if layer == "L0" else causal[:]
                        ins = nc.vector.tensor_tensor_reduce(out=probs[:, q % 4, j, :],
                                                             in0=s_bank[q % 2][:, j * P:j * P + P], in1=more,
                                                             scale=-1.0, scalar=3.0e38, op0=ALU.add, op1=ALU.min,
                                                             accum_out=nmx[:, q % 4, j:j + 1])
                else:
                    ins = nc.vector.tensor_reduce(nmx[:, q % 4, :], s_bank[q % 2][:].rearrange("p (j k) -> p j k", j=4),
                                                  AX.X, ALU.max, negate=True)
                ins.then_inc(maxed, 1)

            dve.wait_ge(set_up_dve, 2)
            dve.wait_ge(set_up, 3)
            with dve.Fori(0, NG) as i:
                turn(i)

            dve.wait_ge(prog_meant, 1)
            nc.vector.tensor_copy(means[SS:P, :], o_bank[SS:P, 0:B]).then_inc(means_ready, 1)
            dve.wait_ge(means_ready, 1)
            nc.vector.tensor_copy(stT[SS:P, :, :], means[SS:P, :].unsqueeze(2).broadcast_to([SS, B, P]))\
                .then_inc(means_ready, 1)
            for n in range(B // PAIR):
                dve.wait_ge(last_filled, n + 1)
                x7 = x7_all[:, PAIR * n:PAIR * n + PAIR, :]
                nc.vector.tensor_tensor(x7, d_bank[n % NB][:].rearrange("p (b n) -> p b n", b=PAIR), x7, ALU.add)\
                    .then_inc(last_added, 1)

        @block.scalar
        def _(act):
            def dense_ready(i, *step):
                slot, n = dense_slot(step)
                act.wait_ge(filled[slot], i * ND + n + 1)
                return d_bank[slot], drained[slot]

            def turn(i):
                for step in STEPS:
                    kind, key = step[0], step[1]
                    p = step[2] if len(step) > 2 else 0
                    if kind == "score":
                        layer, b, c = QUADS[key]
                        act.wait_ge(maxed, quads_done(i, key) + LEAD["quads"])
                        for j in range(4):
                            src = probs[:, key % 4, j, :] if layer in BIASED else s_bank[key % 2][:, j * P:j * P + P]
                            scale = -1.0 if layer in BIASED else 1.0
                            ins = nc.scalar.activation(probs[:, key % 4, j, :], src, ACT.Exp,
                                                       bias=nmx[:, key % 4, j:j + 1], scale=scale,
                                                       accum_out=total[:, key % 4, j:j + 1])
                        ins.then_inc(exped, 1)
                    elif kind == "mix" and QUADS[key][0] == "L1a":
                        act.wait_ge(mixed, quads_done(i, key) + LEAD["mixed"])
                        nc.scalar.activation(h4[0:4, 0:PT], o_bank[0:4, 0:PT], ACT.Gelu, bias=fc1_b[:])\
                            .then_inc(o_copied, 1)
                        nc.scalar.activation(h4[0:4, PT:], o_bank[0:4, PT:], ACT.Gelu, bias=fc1_b[:])\
                            .then_inc(o_copied, 1)
                    elif kind == "flip" and key in ("c", "x4"):
                        d, done = dense_ready(i, *step)
                        dst = cT if key == "c" else actT
                        nc.scalar.copy(dst[:, :, PT * p:PT * p + PT], d[:].rearrange("p (c t) -> p c t", c=DC))\
                            .then_inc(done, 1)
                    elif kind == "flip" and key == "cn":
                        d, done = dense_ready(i, *step)
                        for dst, g, b in ((n1T, "L1_n1w", "L1_n1b"), (n3T, "L3_g1", "L3_be1")):
                            for c in range(DC):
                                ins = nc.scalar.activation(toks(dst, c, p), d[:, c * PT:c * PT + PT], ACT.Identity,
                                                           bias=col(b, c), scale=col(g, c))
                        ins.then_inc(done, 1)
                    elif kind == "k":
                        d, done = dense_ready(i, *step)
                        for c in range(DC):
                            if key == "L3":
                                ins = nc.scalar.activation(toks(k3T, c, p), d[:, c * PT:c * PT + PT],
                                                           ACT.Identity, bias=col("L3_bk", c))
                                continue
                            l = ("L0", "L2").index(key)
                            for h in range(2):
                                ins = nc.scalar.activation(toks(kT[:, h], c, p), d[:, c * PT:c * PT + PT],
                                                           ACT.Identity, bias=bk_half[:, l, h, c:c + 1],
                                                           scale=masks[:, 8 + h:9 + h])
                        ins.then_inc(done, 1)
                    elif kind == "q":
                        d, done = dense_ready(i, *step)
                        for c in range(DC):
                            ins = nc.scalar.activation(qs[:, p, c, :], d[:, c * PT:c * PT + PT], ACT.Identity,
                                                       bias=col(f"{key}_bq", c))
                        ins.then_inc(done, 1)
                    elif kind == "v" and key == "L1":
                        d, done = dense_ready(i, *step)
                        nc.scalar.copy(v1[:], d[:, 0:4 * G].rearrange("p (b n) -> p b n", b=G)).then_inc(done, 1)
                    elif kind == "v" and key == "L3":
                        d, done = dense_ready(i, *step)
                        nc.scalar.copy(pair(v3, p), d[:].rearrange("p (b n) -> p b n", b=PAIR)).then_inc(done, 1)
                    elif kind == "cross":
                        d, done = dense_ready(i, *step)
                        nc.scalar.copy(pair(cr, p), d[:].rearrange("p (b n) -> p b n", b=PAIR)).then_inc(done, 1)
                    elif kind == "ffn1" and key == "L2":
                        d, done = dense_ready(i, *step)
                        for m in range(2):
                            k = 2 * step[3] + m
                            ins = nc.scalar.activation(hT[:, p, k, :], d[:, m * PT:m * PT + PT], ACT.Gelu,
                                                       bias=col("L2_b1", k))
                        ins.then_inc(done, 1)

            act.wait_ge(first_loaded, 16 * len(FIRST_LOADS))
            act.wait_ge(set_up_dve, 1)
            act.wait_ge(set_up, 3)
            with act.Fori(0, NG) as i:
                turn(i)

            z = [s_bank[0], s_bank[1], t_bank[0], t_bank[1]]
            act.wait_ge(stepped, 1)
            nc.scalar.mul(w_state[:, 0, :], u_all[:, 0, :], 0.0)
            for t in range(1, P):
                act.wait_ge(stepped, t)
                nc.scalar.activation(w_state[:, t, :], z[t // 32][0:SS, (t % 32) * B:(t % 32) * B + B], ACT.Silu)\
                    .then_inc(silued, 1)


def _columns(inputs):
    import numpy as np
    n = lambda k: np.asarray(inputs[k])
    bqkv = n("L3_xattn_b_qkv")
    vecs = {"L0_g1": n("L0_xattn_g1"), "L0_be1": n("L0_xattn_be1"), "L0_bq": n("L0_xattn_bq"),
            "L0_bk": n("L0_xattn_bk"), "L0_bv": n("L0_xattn_bv"), "L0_g2": n("L0_xattn_g2"),
            "L0_be2": n("L0_xattn_be2"), "L0_b1": n("L0_xattn_b1"), "L1_n1w": n("L1_xattn_norm1_w"),
            "L1_n1b": n("L1_xattn_norm1_b"), "L1_n2w": n("L1_xattn_norm2_w"), "L1_n2b": n("L1_xattn_norm2_b"),
            "L1_n3w": n("L1_xattn_norm3_w"), "L1_n3b": n("L1_xattn_norm3_b"), "L2_bq": n("L2_xattn_bq"),
            "L2_bk": n("L2_xattn_bk"), "L2_bv": n("L2_xattn_bv"), "L2_b1": n("L2_xattn_b1"),
            "L2_g": n("L2_xattn_ln_g"), "L2_b": n("L2_xattn_ln_b"), "L3_g1": n("L3_xattn_g1"),
            "L3_be1": n("L3_xattn_beta1"), "L3_bq": bqkv[0:D], "L3_bk": bqkv[D:2 * D], "L3_bv": bqkv[2 * D:3 * D],
            "L3_g2": n("L3_xattn_g2"), "L3_be2": n("L3_xattn_beta2"), "L3_bin": n("L3_xattn_b_in")}
    return np.ascontiguousarray(np.concatenate([vecs[k].reshape(-1, P).T for k in COLS], axis=1))


def _arrays(inputs):
    import numpy as np
    n = lambda k: np.asarray(inputs[k])

    def lhs(w):
        return np.ascontiguousarray(w.T.reshape(-1, P, w.shape[0]).transpose(1, 0, 2))

    def rhs(w):
        return np.ascontiguousarray(w.reshape(-1, P, w.shape[1]).transpose(1, 0, 2))

    r = {"bo_bg": "L0_xattn_bo", "bg": "L0_xattn_bg", "L0_b2": "L0_xattn_b2", "n2w": "L1_xattn_norm2_w",
         "n2b_all": "L1_xattn_norm2_b", "gamma2": "L1_xattn_gamma2", "gamma1": "L1_xattn_gamma1",
         "n3w": "L1_xattn_norm3_w", "n3b": "L1_xattn_norm3_b", "L2_g": "L2_xattn_ln_g", "L2_b_b2": "L2_xattn_ln_b",
         "L2_b2": "L2_xattn_b2", "L3_bo": "L3_xattn_b_o", "b_prog": "L3_xattn_b_prog"}
    qkv = n("L3_xattn_W_qkv")
    part = np.arange(P)
    masks = np.zeros((P, 10), np.float32)
    for half in range(2):
        masks[part // 64 == half, 8 + half] = 1.0
    for v in range(4):
        masks[(part % 64) // 16 == v, v] = 16 ** -0.5
        masks[part // 32 == v, 4 + v] = 32 ** -0.5
    return {
        "x": n("x"), "ctx": n("ctx_1024"), "mask": n("mask_BxSxS2_fk0"), "prog": n("ctxb_2048x64"),
        "cols": _columns(inputs),
        "rows": np.ascontiguousarray(np.concatenate([n(r[k]) for k in ROWS])[None, :]),
        "ident": np.eye(P, dtype=np.float32), "masks": masks,
        "causal": np.where(np.tril(np.ones((P, P), bool)), 0.0, NEG).astype(np.float32),
        "L0_wq": lhs(n("L0_xattn_Wq")), "L0_wk": lhs(n("L0_xattn_Wk")), "L0_wv": lhs(n("L0_xattn_Wv")),
        "L0_wo": lhs(n("L0_xattn_Wo")), "L0_wg": lhs(n("L0_xattn_Wg")), "L0_w1": lhs(n("L0_xattn_W1")),
        "L0_w2": lhs(n("L0_xattn_W2")), "L1_fc1": lhs(n("L1_xattn_fc1_w")),
        "fc1_b": np.ascontiguousarray(n("L1_xattn_fc1_b")[:, None]),
        "fc2": np.ascontiguousarray(n("L1_xattn_fc2_w").T), "fc2_b": np.ascontiguousarray(n("L1_xattn_fc2_b")[None, :]),
        "L2_wq": lhs(n("L2_xattn_Wq")), "L2_wk": lhs(n("L2_xattn_Wk")), "L2_wv": lhs(n("L2_xattn_Wv")),
        "L2_w1": lhs(n("L2_xattn_W1")), "L2_w2": lhs(n("L2_xattn_W2")),
        "L3_wq": lhs(qkv[0:D]), "L3_wk": lhs(qkv[D:2 * D]), "L3_wv": lhs(qkv[2 * D:3 * D]),
        "L3_wo": lhs(n("L3_xattn_W_o")), "L3_w_in": rhs(n("L3_xattn_W_in")), "L3_bmat": rhs(n("L3_xattn_Bmat")),
        "a_t": np.ascontiguousarray(n("L3_xattn_A").T), "cmat": n("L3_xattn_Cmat"),
        "wprog": np.ascontiguousarray(n("L3_xattn_W_prog").T),
    }


def kernel(**inputs):
    import numpy as _np
    import concourse.bacc as _bacc
    from concourse.bass_utils import run_bass_kernel_spmd as _run

    nc = _bacc.Bacc("TRN2", target_bir_lowering=False, num_devices=1)
    arrays = {f"in_{k}": v for k, v in _arrays(inputs).items()}
    a = {k[3:]: nc.dram_tensor(k, v.shape, mybir.dt.from_np(v.dtype), kind="ExternalInput").ap()
         for k, v in arrays.items()}
    out = nc.dram_tensor("out_0", (B, P, D), F32, kind="ExternalOutput").ap()
    network(nc, a, out)
    r = _run(nc, [arrays], core_ids=[0])
    return r.results[0]["out_0"]
```

```python
from contextlib import ExitStack

import concourse.bass as bass
from concourse import mybir

ALU = mybir.AluOpType
ACT = mybir.ActivationFunctionType
AX = mybir.AxisListType
F32 = mybir.dt.float32
BF16 = mybir.dt.bfloat16

P = 128
B = 16
D = 256
DC = D // P
FF = 1024
FC = FF // P
PAIR = 2
NT = B // PAIR
PT = PAIR * P
H16, H8 = 16, 8
SS = 64
PP = 64
EPS = 1e-5
NEG = -1e9

COLS = {}
_at = 0
for _name, _n in [("L0_g1", 2), ("L0_be1", 2), ("L0_bq", 2), ("L0_bk", 2), ("L0_bv", 2), ("L0_g2", 2), ("L0_be2", 2),
                  ("L0_b1", 8), ("L1_n1w", 2), ("L1_n1b", 2), ("L1_n2w", 2), ("L1_n2b", 2), ("L1_n3w", 2),
                  ("L1_n3b", 2), ("L2_bq", 2), ("L2_bk", 2), ("L2_bv", 2), ("L2_b1", 8), ("L2_g", 2), ("L2_b", 2),
                  ("L3_g1", 2), ("L3_be1", 2), ("L3_bq", 2), ("L3_bk", 2), ("L3_bv", 2), ("L3_g2", 2),
                  ("L3_be2", 2), ("L3_bin", 2)]:
    COLS[_name] = _at
    _at += _n
NCOL = _at
ROWS = {n: k for k, n in enumerate(["bo_bg", "bg", "L0_b2", "n2w", "n2b_all", "gamma2", "gamma1", "n3w", "n3b",
                                    "L2_g", "L2_b_b2", "L2_b2", "L3_bo", "b_prog"])}

QUADS = {"A": [("L0", b, c) for b in range(PAIR) for c in range(4)] + [("L1a", 0, 0), ("L1b", 0, 0)],
         "B": [("L2", b, c) for b in range(PAIR) for c in range(4)] + [("L3", b, c) for b in range(PAIR) for c in range(2)],
         "H": []}
NQ = {s: len(q) for s, q in QUADS.items()}
PROBS = 4


ORDER = """
B:flip.x4 B:q.L2 B:v.L2 B:k.L2 B:k.L3 A:stat.c B:score.0 B:score.1 B:sums.0 A:score.0 B:score.2 B:sums.1 A:score.1
B:turn.0 B:v.L3 A:sums.0 B:sums.2 B:score.3 A:score.2 B:mix.0 A:norm.c B:turn.1 B:score.4 A:sums.1 A:turn.0 B:sums.3
A:sums.2 B:mix.1 B:turn.2 A:score.3 A:flip.c B:score.5 A:mix.0 B:mix.2 A:score.4 B:sums.4 A:turn.1 B:turn.3
B:score.6 A:mix.1 A:sums.3 A:flip.cn B:mix.3 A:score.5 B:sums.5 B:turn.4 B:score.7 A:turn.2 B:mix.4 B:sums.6
B:turn.5 B:sums.7 A:sums.4 B:mix.5 A:mix.2 B:turn.6 A:sums.5 A:v.L1 A:turn.3 A:score.6 B:mix.6 B:turn.7 B:mix.7
A:turn.4 B:flip.o B:stat.x5 A:mix.3 A:sums.6 B:norm.x5 A:score.7 A:mix.4 A:turn.5 B:flip.x5 A:sums.7 A:mix.5
A:turn.6 B:ffn1.L2.0 A:turn.7 A:mix.6 B:ffn1.L2.1 A:mix.7 B:ffn1.L2.2 B:ffn1.L2.3 A:out.L0 A:stat.x2 A:norm.x2
B:ffn2.L2 A:flip.x2 B:stat.x6 B:norm.x6 A:ffn1.L0.0 A:ffn1.L0.1 B:flip.x6 A:ffn1.L0.2 A:ffn1.L0.3 B:q.L3 A:ffn2.L0
B:score.8 A:stat.x3 A:norm.x3 H:stat.x B:score.9 A:flip.x3 B:sums.8 B:score.10 B:sums.9 A:score.8 H:norm.x B:turn.8
A:sums.8 H:flip.x B:sums.10 B:score.11 B:turn.9 B:mix.8 A:turn.8 B:sums.11 B:turn.10 B:mix.9 A:mix.8 B:mix.10
B:turn.11 A:cross.L1 B:mix.11 A:stat.cr H:q.L0 H:v.L0 A:norm.cr B:out.L3 A:flip.cr B:stat.x7 A:score.9 H:k.L0
A:sums.9 B:norm.x7 A:turn.9 B:flip.x7 A:self.L1 B:drive.L3
"""


def parse(order):
    out = []
    for word in order.split():
        stream, step = word.split(":")
        out.append((stream, tuple(int(x) if x.isdigit() else x for x in step.split("."))))
    return out


WOVEN = parse(ORDER)
STEPS = {s: [x for t, x in WOVEN if t == s] for s in "ABH"}
assert WOVEN.index(("B", ("v", "L2"))) < WOVEN.index(("B", ("k", "L2"))) < WOVEN.index(("A", ("flip", "c")))
assert WOVEN.index(("B", ("v", "L3"))) < WOVEN.index(("A", ("flip", "cn")))
DENSE_KINDS = ("flip", "q", "k", "v", "out", "ffn1", "ffn2", "cross", "self", "drive")


def bank_of(step):
    kind, key = step[:2]
    if kind in ("q", "k") and key == "L0":
        return "o"
    return "t" if kind == "q" or (kind == "k" and key != "L3") or (kind == "ffn1" and step[2] % 2 == 0) else "d"


DENSE = {s: [x for x in STEPS[s] if x[0] in DENSE_KINDS] for s in "ABH"}
STATS = {s: [x[1] for x in STEPS[s] if x[0] == "stat"] for s in "ABH"}
FLIPPED = {s: [x[1] for x in STEPS[s] if x[0] == "flip" and x[1] in ("x", "x2", "x3", "cr", "x5", "x6", "x7")]
           for s in "ABH"}
MASKED = {s: [x[1] for x in STEPS[s] if x[0] == "q"] for s in "ABH"}
POOL_JOBS = {"A": ["xb", "x2b", "skip"], "B": ["x5b", "x6b", "x7b"]}
DVE_LINKS = {"A": 2 * len(STATS["A"]) + 1, "B": 2 * len(STATS["B"]), "H": 2 * len(STATS["H"]) + 1}
POOL_LINKS = {"A": 3, "B": 1, "H": 0}
O_USES = {"A": [("L0", 0), ("L0", 1), ("L1a", 0)], "B": [("L2", 0), ("L2", 1), ("L3", 0), ("L3", 1)]}


class Stream:

    def __init__(self, name, sb, bank, sem):
        self.name = name
        self.s_bank = bank(f"{name}_scores_bank")
        self.t_bank = bank(f"{name}_turned_bank")
        self.o_bank = bank(f"{name}_mixed_bank")
        self.d_bank = bank(f"{name}_dense_bank")
        self.xn = sb(f"{name}_xn", [P, PAIR, D])
        self.cur = sb(f"{name}_cur", [P, PAIR, D])
        self.res = sb(f"{name}_res", [P, PAIR, D])
        self.actT = sb(f"{name}_actT", [P, DC, PT])
        self.wide = sb(f"{name}_wide", [P, FC * PT])
        self.qm = self.wide[:].rearrange("p (v c t) -> p v c t", v=4, c=DC)
        self.hT = self.wide[:].rearrange("p (k t) -> p k t", k=FC)
        self.kT = sb(f"{name}_kT", [P, 2, DC, PT])
        self.vpad = sb(f"{name}_vpad", [P, PAIR, H16 // 2, 64])
        self.oT = sb(f"{name}_oT", [P, DC, PT])
        self.probs = sb(f"{name}_probs", [P, PROBS, 4, P])
        self.probsT = sb(f"{name}_probsT", [P, 2, 4, P])
        self.nmx = sb(f"{name}_nmx", [P, PROBS, 4])
        self.total = sb(f"{name}_total", [P, PROBS, 4])
        self.rtotal = sb(f"{name}_rtotal", [P, PROBS, 4])
        self.stats = sb(f"{name}_stats", [P, PAIR, 6])
        self.moments = sb(f"{name}_moments", [P, PAIR, 2])
        self.veps = sb(f"{name}_veps", [P, PAIR])
        self.rstd = sb(f"{name}_rstd", [P, PAIR])
        self.scored = sem(f"{name}_scored")
        self.maxed = sem(f"{name}_maxed")
        self.exped = sem(f"{name}_exped")
        self.rsummed = sem(f"{name}_rsummed")
        self.weighed = sem(f"{name}_weighed")
        self.turned = sem(f"{name}_turned")
        self.copied = sem(f"{name}_copied")
        self.mixed = sem(f"{name}_mixed")
        self.o_copied = sem(f"{name}_o_copied")
        self.filled = sem(f"{name}_filled")
        self.drained = {"d": sem(f"{name}_dense_drained"), "t": sem(f"{name}_turned_drained")}
        self.flipped = sem(f"{name}_flipped")
        self.masked = sem(f"{name}_masked")
        self.var_ready = sem(f"{name}_var_ready")
        self.rstd_ready = sem(f"{name}_rstd_ready")
        self.normed = sem(f"{name}_normed")
        self.summed = sem(f"{name}_summed")
        self.dve_link = sem(f"{name}_dve_link")
        self.pool_link = sem(f"{name}_pool_link")

    def quads_at(self, i, q):
        return i * NQ[self.name] + q + 1

    def before(self, step, where):
        return sum(bank_of(x) == where for x in DENSE[self.name][:DENSE[self.name].index(step)])

    def in_bank(self, where):
        return sum(bank_of(x) == where for x in DENSE[self.name])

    def drained_at(self, i, *step):
        where = bank_of(step)
        return self.drained[where], i * self.in_bank(where) + self.before(step, where) + 1 + LEAD["dense"]

    def dense_bank(self, step):
        return {"d": self.d_bank, "t": self.t_bank, "o": self.o_bank}[bank_of(step)]

    def score_bank(self, q):
        return self.d_bank if QUADS[self.name][q][0] == "L3" and q % 2 else self.s_bank

    def masked_at(self, i, layer, chunk):
        return self.masked, (i * len(MASKED[self.name]) + MASKED[self.name].index(layer)) * DC + chunk + 1

    def filled_at(self, i, *step):
        return self.filled, i * len(DENSE[self.name]) + DENSE[self.name].index(step) + 1

    def flipped_at(self, i, key):
        return self.flipped, i * len(FLIPPED[self.name]) + FLIPPED[self.name].index(key) + 1

    def normed_at(self, i, key, b=PAIR - 1):
        return self.normed, (i * len(STATS[self.name]) + STATS[self.name].index(key)) * PAIR + b + 1

    def summed_at(self, i, job):
        return self.summed, i * len(POOL_JOBS[self.name]) + POOL_JOBS[self.name].index(job) + 1

    def o_copied_at(self, i, layer, b):
        uses = O_USES[self.name]
        return self.o_copied, i * len(uses) + uses.index((layer, b)) + 1 + LEAD["o"]


class Head(Stream):

    def __init__(self, of, sb, sem):
        self.name = "H"
        self.d_bank, self.o_bank, self.t_bank = of.d_bank, of.o_bank, of.t_bank
        self.xn, self.cur, self.oT, self.qm, self.kT, self.vpad = of.xn, of.cur, of.oT, of.qm, of.kT, of.vpad
        self.actT = sb("H_actT", [P, DC, PT])
        self.stats = sb("H_stats", [P, PAIR, 6])
        self.moments = sb("H_moments", [P, PAIR, 2])
        self.veps = sb("H_veps", [P, PAIR])
        self.rstd = sb("H_rstd", [P, PAIR])
        self.filled = sem("H_filled")
        self.drained = {"d": sem("H_dense_drained"), "o": sem("H_mixed_drained")}
        self.flipped = sem("H_flipped")
        self.masked = sem("H_masked")
        self.var_ready = sem("H_var_ready")
        self.rstd_ready = sem("H_rstd_ready")
        self.normed = sem("H_normed")
        self.dve_link = sem("H_dve_link")


def last_in_dense(name, i, step):
    users = [(t, x) for t, x in WOVEN if t in "AH" and x[0] in DENSE_KINDS and bank_of(x) == "d"]
    at, turn = users.index((name, step)), i - (name == "H")
    for back in range(1, 2 * len(users)):
        t, x = users[(at - back) % len(users)]
        j = turn + (t == "H") - (1 if back > at else 0)
        if not isinstance(j, int) or 0 <= j < NT:
            return t, j, x
        if isinstance(j, int) and back > len(users):
            return None


LEAD = {"scores": 1, "probs": PROBS, "copied": 1, "mixed": 2, "o": 1, "dense": 1}
BIASED = ("L0", "L2")
HEADS_PER_LAYER = {"L0": H16, "L2": H16, "L3": H8}


def network(nc, a, out):
    with ExitStack() as ctx:
        def sb(name, shape, dt=F32):
            return ctx.enter_context(nc.sbuf_tensor(name, shape, dt))

        def bank(name):
            return ctx.enter_context(nc.psum_tensor(name, [P, 512], F32))

        def sem(name):
            return ctx.enter_context(nc.semaphore(name))

        def weight(name, k, n):
            return sb(name, [P, k, n])

        wq = {l: weight(f"{l}_wq", DC, D) for l in ("L0", "L2", "L3")}
        wk = {l: weight(f"{l}_wk", DC, D) for l in ("L0", "L2", "L3")}
        wv = {l: weight(f"{l}_wv", DC, D) for l in ("L0", "L2", "L3")}
        wo = {l: weight(f"{l}_wo", DC, D) for l in ("L0", "L3")}
        wg = weight("L0_wg", DC, D)
        w1 = {l: weight(f"{l}_w1", DC, FF) for l in ("L0", "L2")}
        w2 = {l: weight(f"{l}_w2", FC, D) for l in ("L0", "L2")}
        fc1 = weight("L1_fc1", DC, 4)
        fc2 = sb("L1_fc2", [5, D])
        w_drive = weight("w_drive", DC, SS)
        b_drive = sb("b_drive", [SS, 1])
        bmat = weight("bmat", DC, SS)
        a_t = sb("a_t", [SS, SS])
        w_last = sb("w_last", [P, D])
        cols = sb("cols", [P, NCOL])
        fc1_b = sb("fc1_b", [4, 1])
        rows = sb("rows", [P, len(ROWS), D])
        ident = sb("ident", [P, P])
        masks = sb("masks", [P, 4 + 4 + 2])
        bk_half = sb("bk_half", [P, 2, 2, DC])
        causal = sb("causal", [P, P])
        half = sb("half", [P, PAIR])
        mean_w = sb("mean_w", [P, 1])

        x_in = sb("x_in", [P, PAIR, D])
        c_in = sb("c_in", [P, PAIR, D])
        cn = sb("cn", [P, PAIR, D])
        bias = sb("bias", [P, PAIR, P])
        cT = sb("cT", [P, DC, PT])
        n1T = sb("n1T", [P, DC, PT])
        n3T = sb("n3T", [P, DC, PT])
        xl = {"x3": sb("xn3", [P, PAIR, D]), "x5": sb("xn5", [P, PAIR, D])}
        cr = sb("cr", [P, PAIR, D])
        v1 = sb("v1", [P, PAIR, 4])
        h4 = sb("h4", [5, PT])
        x4 = sb("x4", [P, PAIR, D])
        k3T = sb("k3T", [P, DC, PT])
        v3 = sb("v3", [P, PAIR, D])
        x7_all = sb("x7_all", [P, B, D])
        u_all = sb("u_all", [SS, P, B])

        A, Bs = Stream("A", sb, bank, sem), Stream("B", sb, bank, sem)
        Hd = Head(A, sb, sem)
        streams = {"A": A, "B": Bs, "H": Hd}

        w_in = Bs.wide[:, 0:DC * D].rearrange("p (k n) -> p k n", k=DC)
        w_state = A.wide[0:SS, :].rearrange("p (t b) -> p t b", b=B)
        prog = Bs.wide[:, 0:B * PP].rearrange("p (b s) -> p b s", b=B)
        stT = Bs.wide[:].rearrange("p (b t) -> p b t", b=B)
        means = sb("means", [P, B])

        first_loaded, rows_loaded = sem("first_loaded"), sem("rows_loaded")
        l0_loaded, rest_loaded = sem("l0_loaded"), sem("rest_loaded")
        x_loaded, c_loaded, prog_loaded = sem("x_loaded"), sem("c_loaded"), sem("prog_loaded")
        out_stored = sem("out_stored")
        set_up = sem("set_up")
        set_up_dve = sem("set_up_dve")
        set_up_pe = sem("set_up_pe")
        dve_waited = sem("dve_waited")
        stepped, silued = sem("stepped"), sem("silued")
        prog_meant, means_ready = sem("prog_meant"), sem("means_ready")
        states_ready, last_filled, last_added = sem("states_ready"), sem("last_filled"), sem("last_added")

        def rows_over(name, n=PAIR):
            return rows[:, ROWS[name]:ROWS[name] + 1, :].broadcast_to([P, n, D])

        def row(name):
            return rows[:, ROWS[name], :]

        def col(name, c):
            return cols[:, COLS[name] + c:COLS[name] + c + 1]

        def by_batch(d):
            return d[:].rearrange("p (b n) -> p b n", b=PAIR)

        FIRST_LOADS = [(ident[:], a["ident"]), (cols[:], a["cols"]), (masks[:], a["masks"]),
                       (wq["L0"][:], a["L0_wq"]), (wv["L0"][:], a["L0_wv"]), (wk["L0"][:], a["L0_wk"])]
        L0_LOADS = [(fc1[:], a["L1_fc1"]), (fc1_b[:], a["fc1_b"]), (wo["L0"][:], a["L0_wo"]), (wg[:], a["L0_wg"]), (w1["L0"][:], a["L0_w1"]), (w2["L0"][:], a["L0_w2"]),
                    (fc2[0:4, :], a["fc2"]), (fc2[4:5, :], a["fc2_b"])]
        REST_LOADS = [(w_in, a["L3_w_in"]), (bmat[:], a["L3_bmat"]), (causal[:], a["causal"]), (a_t[:], a["a_t"]),
                      (wk["L2"][:], a["L2_wk"]), (wv["L2"][:], a["L2_wv"]), (wk["L3"][:], a["L3_wk"]),
                      (wv["L3"][:], a["L3_wv"]),
                      (wq["L2"][:], a["L2_wq"]), (w1["L2"][:], a["L2_w1"]), (w2["L2"][:], a["L2_w2"]),
                      (wq["L3"][:], a["L3_wq"]), (wo["L3"][:], a["L3_wo"]), (w_last[0:SS, :], a["cmat"]),
                      (w_last[SS:P, :], a["wprog"])]

        def turns(eng, turn, between=lambda: None):
            turn({"H": 0})
            turn({"A": 0, "H": 1})
            between()
            with eng.Fori(1, NT - 1) as i:
                turn({"A": i, "B": i - 1, "H": i + 1})
            turn({"A": NT - 1, "B": NT - 2})
            turn({"B": NT - 1})

        def live(index):
            return [(streams[s], index[s], step) for s, step in WOVEN if s in index]

        block = ctx.enter_context(nc.Block())

        @block.sync
        def _(sp):
            def load_x(i):
                sp.dma_start(x_in[:], a["x"][bass.ds(i * PAIR, PAIR)].rearrange("b s d -> s b d"))\
                    .then_inc(x_loaded, 16)

            def load_c(i):
                sp.dma_start(c_in[:], a["ctx"][bass.ds(i * PAIR, PAIR)].rearrange("b s d -> s b d"))\
                    .then_inc(c_loaded, 16)
                sp.dma_start(bias[:], a["mask"][bass.ds(i * PAIR, PAIR)].rearrange("b q k -> q b k"))\
                    .then_inc(c_loaded, 16)

            load_x(0)
            for t, src in FIRST_LOADS:
                sp.dma_start(t, src).then_inc(first_loaded, 16)
            load_c(0)
            sp.dma_start(rows[:].rearrange("p r d -> p (r d)"), a["rows"].broadcast_to([P, len(ROWS) * D]))\
                .then_inc(rows_loaded, 16)
            for t, src in L0_LOADS:
                sp.dma_start(t, src).then_inc(l0_loaded, 16)
            for t, src in REST_LOADS:
                sp.dma_start(t, src).then_inc(rest_loaded, 16)
            with sp.Fori(1, NT) as i:
                sp.wait_ge(*A.summed_at(i - 1, "xb"))
                sp.wait_ge(*Hd.normed_at(i - 1, "x"))
                load_x(i)
                sp.wait_ge(*A.normed_at(i - 1, "c"))
                sp.wait_ge(*A.filled_at(i - 1, "flip", "c"))
                sp.wait_ge(A.maxed, A.quads_at(i - 1, 7) + LEAD["scores"])
                load_c(i)
            sp.wait_ge(*Bs.drained_at(NT - 1, "drive", "L3"))
            sp.dma_start(prog, a["prog"].rearrange("b s k -> s b k")).then_inc(prog_loaded, 16)
            with sp.Fori(0, B // PAIR) as j:
                sp.wait_ge(last_added, j + 1)
                sp.dma_start(out[bass.ds(j * PAIR, PAIR)].rearrange("b s d -> s b d"),
                             x7_all[:, bass.ds(j * PAIR, PAIR), :]).then_inc(out_stored, 16)
            sp.wait_ge(out_stored, 16 * (B // PAIR))

        @block.tensor
        def _(pe):
            def dense(s, i, step):
                where = bank_of(step)
                if where == "d" and s is not Bs:
                    last = last_in_dense(s.name, i, step)
                    if last:
                        t, j, x = last
                        pe.wait_ge(*streams[t].drained_at(j, *x))
                elif where == "o" and step[0] == "q":
                    if not isinstance(i, int) or i > 0:
                        pe.wait_ge(*A.o_copied_at(i - 1, "L1a", 0))
                else:
                    pe.wait_ge(s.drained[where], i * s.in_bank(where) + s.before(step, where) + LEAD["dense"])
                return s.dense_bank(step)

            def flip(s, i, key):
                src = {"x": s.xn, "x2": s.xn, "x6": s.xn, "x7": s.xn, "x3": xl["x3"], "x5": xl["x5"], "c": c_in,
                       "cn": cn, "cr": cn, "x4": x4}.get(key)
                if key == "c":
                    pe.wait_ge(c_loaded, i * 32 + 32)
                elif key == "x4":
                    pe.wait_ge(rest_loaded, 16 * len(REST_LOADS))
                    pe.wait_ge(*A.drained_at(i, "self", "L1"))
                elif key == "o":
                    pe.wait_ge(*s.o_copied_at(i, "L2", PAIR - 1))
                d = dense(s, i, ("flip", key))
                for b in range(PAIR):
                    if key not in ("c", "x4", "o"):
                        pe.wait_ge(*s.normed_at(i, "c" if key == "cn" else key, b))
                    for c in range(DC):
                        if key == "o":
                            mm = nc.tensor.transpose(d[:, b * D + c * P:b * D + c * P + P],
                                                     s.oT[:, c, b * P:b * P + P], ident[:])
                        else:
                            mm = nc.tensor.transpose(d[:, c * PT + b * P:c * PT + b * P + P],
                                                     src[:, b, c * P:c * P + P], ident[:])
                mm.then_inc(s.filled, 1)

            def project(s, i, step, w, xT, m0=0, flipped=None):
                d = dense(s, i, step)
                for m in range(2):
                    for k in range(DC):
                        if flipped and m == 0:
                            pe.wait_ge(*(s.drained_at(i, "flip", flipped) if k else s.flipped_at(i, flipped)))
                        mm = nc.tensor.matmul(d[:, m * PT:m * PT + PT], w[:, k, (m0 + m) * P:(m0 + m) * P + P],
                                              xT[:, k, :], start=(k == 0), stop=(k == DC - 1))
                mm.then_inc(s.filled, 1)

            def project_rows(s, i, step, *terms):
                d = dense(s, i, step)
                for b in range(PAIR):
                    todo = [(xT[:, k, b * P:b * P + P], w[:, k, :]) for xT, w in terms for k in range(w.shape[1])]
                    for n, (xT, w) in enumerate(todo):
                        mm = nc.tensor.matmul(d[:, b * D:b * D + D], xT, w, start=(n == 0), stop=(n == len(todo) - 1))
                mm.then_inc(s.filled, 1)

            def scores(s, i, q):
                layer, b, c = QUADS[s.name][q]
                last = q - 2 if layer == "L3" and q >= NQ["B"] - 2 else q - 1
                if s.score_bank(q) is s.s_bank or last == q - 2:
                    pe.wait_ge(s.maxed if QUADS[s.name][last][0] in BIASED else s.exped,
                               s.quads_at(i, q) - (q - last) + LEAD["scores"])
                own = Hd if layer == "L0" else s
                if layer in ("L0", "L2", "L3"):
                    pe.wait_ge(*own.drained_at(i, "k", layer))
                    pe.wait_ge(*own.masked_at(i, layer, c if layer == "L3" else c // 2))
                    for j in range(4):
                        if layer == "L3":
                            ops = s.qm[:, j, c, b * P:b * P + P], k3T[:, c, b * P:b * P + P]
                        else:
                            ops = s.qm[:, j, c // 2, b * P:b * P + P], s.kT[:, c % 2, c // 2, b * P:b * P + P]
                        mm = nc.tensor.matmul(s.score_bank(q)[:, j * P:j * P + P], *ops, start=True, stop=True)
                else:
                    keysT = n1T if layer == "L1a" else s.actT
                    flipped = "x3" if layer == "L1a" else "cr"
                    for j in range(PAIR):
                        for k in range(DC):
                            if j == 0:
                                pe.wait_ge(*(s.drained_at(i, "flip", flipped) if k else s.flipped_at(i, flipped)))
                            mm = nc.tensor.matmul(s.s_bank[:, j * P:j * P + P], s.actT[:, k, j * P:j * P + P],
                                                  keysT[:, k, j * P:j * P + P], start=(k == 0), stop=(k == DC - 1))
                mm.then_inc(s.scored, 1)

            def mix(s, i, q):
                layer, b, c = QUADS[s.name][q]
                pe.wait_ge(s.copied, s.quads_at(i, q) + LEAD["copied"])
                pT = s.probsT[:, q % 2]
                if c == 0:
                    own, n = s.o_copied_at(i, layer, b)
                    pe.wait_ge(own, n - 1)
                    values = Hd if layer == "L0" else s
                    pe.wait_ge(*values.drained_at(i, "v", "L1" if layer == "L1a" else layer))
                for j in range(PAIR if layer == "L1a" else 4):
                    if layer == "L1a":
                        mm = nc.tensor.matmul(s.o_bank[0:4, j * P:j * P + P], v1[:, j, :], pT[:, j, :],
                                              start=True, stop=True)
                    elif layer == "L3":
                        mm = nc.tensor.matmul(s.o_bank[32 * j:32 * j + 32, c * P:c * P + P],
                                              v3[:, b, (4 * c + j) * 32:(4 * c + j) * 32 + 32], pT[:, j, :],
                                              start=True, stop=True)
                    else:
                        h = 4 * c + j
                        lo = 32 * ((h % 8) // 2)
                        mm = nc.tensor.matmul(s.o_bank[lo:lo + 32, (c // 2) * P:(c // 2) * P + P],
                                              s.vpad[:, b, h // 2, 32 * (h % 2):32 * (h % 2) + 32], pT[:, j, :],
                                              start=(j % 2 == 0), stop=(j % 2 == 1))
                mm.then_inc(s.mixed, 1)

            pe.wait_ge(first_loaded, 16 * len(FIRST_LOADS))

            def drive_weight():
                pe.wait_ge(rest_loaded, 16 * len(REST_LOADS))
                for m in range(DC):
                    for k in range(DC):
                        nc.tensor.matmul(Bs.o_bank[:, m * SS:m * SS + SS], w_in[:, k, m * P:m * P + P], bmat[:, k, :],
                                         start=(k == 0), stop=(k == DC - 1))
                for k in range(DC):
                    mm = nc.tensor.matmul(Bs.o_bank[0:SS, 128:129], bmat[:, k, :], col("L3_bin", k),
                                          start=(k == 0), stop=(k == DC - 1))
                mm.then_inc(set_up_pe, 1)
                pe.wait_ge(set_up_dve, 2)

            def turn(index):
                for s, i, step in live(index):
                    kind, key = step[0], step[1]
                    if kind == "flip":
                        flip(s, i, key)
                    elif kind == "q":
                        if key == "L2":
                            pe.wait_ge(*s.drained_at(i, "flip", "x4"))
                        project(s, i, step, wq[key], s.actT, flipped={"L0": "x", "L3": "x6"}.get(key))
                    elif kind == "k":
                        project(s, i, step, wk[key], {"L0": s.actT, "L2": cT, "L3": n3T}[key])
                    elif kind == "v" and key == "L1":
                        pe.wait_ge(l0_loaded, 16 * len(L0_LOADS))
                        d = dense(s, i, step)
                        for b in range(PAIR):
                            for k in range(DC):
                                mm = nc.tensor.matmul(d[:, 4 * b:4 * b + 4], n1T[:, k, b * P:b * P + P], fc1[:, k, :],
                                                      start=(k == 0), stop=(k == DC - 1))
                        mm.then_inc(s.filled, 1)
                    elif kind == "v":
                        project_rows(s, i, step, ({"L0": s.actT, "L2": cT, "L3": n3T}[key], wv[key]))
                    elif kind == "score":
                        scores(s, i, key)
                    elif kind == "turn":
                        pe.wait_ge(s.weighed, s.quads_at(i, key))
                        pe.wait_ge(s.copied, s.quads_at(i, key) - 1 + LEAD["copied"])
                        for j in range(PAIR if QUADS[s.name][key][0] in ("L1a", "L1b") else 4):
                            mm = nc.tensor.transpose(s.t_bank[:, j * P:j * P + P], s.probs[:, key % PROBS, j, :],
                                                     ident[:])
                        mm.then_inc(s.turned, 1)
                    elif kind == "mix":
                        mix(s, i, key)
                    elif kind == "out":
                        pe.wait_ge(*s.o_copied_at(i, key, PAIR - 1))
                        if key == "L0":
                            pe.wait_ge(l0_loaded, 16 * len(L0_LOADS))
                            project_rows(s, i, step, (s.oT, wo[key]), (cT, wg))
                        else:
                            project_rows(s, i, step, (s.oT, wo[key]))
                    elif kind == "ffn1":
                        project(s, i, step, w1[key], s.actT, 2 * step[2],
                                flipped=None if step[2] else {"L0": "x2", "L2": "x5"}[key])
                    elif kind == "ffn2":
                        pe.wait_ge(*s.drained_at(i, "ffn1", key, FC // 2 - 2))
                        project_rows(s, i, step, (s.hT, w2[key]))
                    elif kind == "cross":
                        pe.wait_ge(*s.o_copied_at(i, "L1a", 0))
                        d = dense(s, i, step)
                        for b in range(PAIR):
                            mm = nc.tensor.matmul(d[:, b * D:b * D + D], h4[:, b * P:b * P + P], fc2[:],
                                                  start=True, stop=True)
                        mm.then_inc(s.filled, 1)
                    elif kind == "self":
                        q = len(QUADS["A"]) - 1
                        pe.wait_ge(s.copied, s.quads_at(i, q) + LEAD["copied"])
                        d = dense(s, i, step)
                        for b in range(PAIR):
                            mm = nc.tensor.matmul(d[:, b * D:b * D + D], s.probsT[:, q % 2, b, :], cn[:, b, :],
                                                  start=True, stop=True)
                        mm.then_inc(s.filled, 1)
                        pe.wait_ge(*s.filled_at(i, *step))
                        pe.sem_inc(s.mixed, 1)
                    elif kind == "drive":
                        d = dense(s, i, step)
                        for k in range(DC):
                            mm = nc.tensor.matmul(d[0:SS, 0:PT], w_drive[:, k, :], s.actT[:, k, :],
                                                  start=(k == 0), stop=(k == DC - 1))
                        mm.then_inc(s.filled, 1)

            turns(pe, turn, drive_weight)

            z = [A.s_bank, A.t_bank, A.o_bank, A.d_bank]
            pe.wait_ge(*Bs.drained_at(NT - 1, "drive", "L3"))
            pe.wait_ge(*A.drained_at(NT - 1, "self", "L1"))
            for n in range(4):
                lo = 32 * n - 1 if n else 0
                dst = z[n][0:SS, 0:512] if n else z[n][0:SS, B:512]
                mm = nc.tensor.matmul(dst, a_t[:], u_all[:, lo:32 * n + 31, :], start=True, stop=(n == 0),
                                      skip_group_check=True)
            for t in range(1, P):
                if t == 2:
                    pe.wait_ge(prog_loaded, 16)
                    for b in range(B):
                        means_mm = nc.tensor.matmul(Bs.o_bank[SS:P, b:b + 1], prog[:, b, :], mean_w[:], start=True,
                                                    stop=True)
                    means_mm.then_inc(prog_meant, 1)
                if t > 1:
                    pe.wait_ge(silued, t - 1)
                    mm = nc.tensor.matmul(z[t // 32][0:SS, (t % 32) * B:(t % 32) * B + B], a_t[:],
                                          w_state[:, t - 1, :], start=False, stop=True, skip_group_check=True)
                mm.then_inc(stepped, 1)

            last_banks = [Bs.s_bank, Bs.t_bank, Bs.d_bank]
            pe.wait_ge(means_ready, 2)
            for n in range(B // PAIR):
                pe.wait_ge(states_ready, n // 2 + 1)
                if n >= 3:
                    pe.wait_ge(last_added, n - 2)
                for b in range(PAIR):
                    mm = nc.tensor.matmul(last_banks[n % 3][:, b * D:b * D + D], stT[:, PAIR * n + b, :], w_last[:],
                                          start=True, stop=True)
                mm.then_inc(last_filled, 1)

        @block.gpsimd
        def _(pool):
            nc.gpsimd.memset(half[:], -0.5)
            nc.gpsimd.memset(mean_w[:], 1.0 / P)
            nc.gpsimd.memset(h4[:], 1.0).then_inc(set_up, 1)
            nc.gpsimd.memset(A.vpad[:], 0.0).then_inc(set_up, 1)
            nc.gpsimd.memset(Bs.vpad[:], 0.0).then_inc(set_up, 1)
            for s in (A, Bs):
                for ring, lead in [(s.maxed, "scores"), (s.exped, "scores"), (s.turned, "probs"), (s.copied, "copied"),
                                   (s.mixed, "mixed"), (s.o_copied, "o"), 
                                   (s.drained["d"], "dense"), (s.drained["t"], "dense")]:
                    pool.sem_inc(ring, LEAD[lead])
            for where in "do":
                pool.sem_inc(Hd.drained[where], LEAD["dense"])

            def add(out, a0, a1, op=ALU.add):
                return nc.gpsimd.tensor_tensor(out, a0, a1, op)

            def combine_rows():
                pool.wait_ge(rows_loaded, 16)
                add(row("bo_bg"), row("bo_bg"), row("bg"))
                add(row("L2_b_b2"), row("L2_b_b2"), row("L2_b2"))
                add(row("gamma1"), row("gamma1"), row("gamma2"), ALU.mult).then_inc(set_up, 1)
                pool.wait_ge(set_up, 4)
                add(row("n3w"), row("n3w"), row("gamma1"), ALU.mult)
                add(row("n3b"), row("n3b"), row("gamma1"), ALU.mult).then_inc(set_up, 1)
                pool.wait_ge(set_up, 5)
                add(row("n2b_all"), row("n2b_all"), row("n3b")).then_inc(set_up, 1)
                pool.wait_ge(set_up, 6)

            def turn(index):
                linked = {"A": 0, "B": 0, "H": 0}

                def link(s, i, ins):
                    linked[s.name] += 1
                    ins.then_inc(s.pool_link, 1)
                    pool.wait_ge(s.pool_link, i * POOL_LINKS[s.name] + linked[s.name])

                for s, i, step in live(index):
                    kind, key = step[0], step[1]
                    if kind == "stat":
                        pool.wait_ge(s.var_ready, i * len(STATS[s.name]) + STATS[s.name].index(key) + 1)
                        add(s.rstd[:], s.veps[:], half[:], ALU.pow).then_inc(s.rstd_ready, 1)
                    if kind == "sums":
                        pool.wait_ge(s.rsummed, s.quads_at(i, key))
                        n = PAIR if QUADS[s.name][key][0] in ("L1a", "L1b") else 4
                        e = s.probs[:, key % PROBS, 0:n, :]
                        add(e, e, s.rtotal[:, key % PROBS, 0:n].unsqueeze(2).broadcast_to([P, n, P]), ALU.mult)\
                            .then_inc(s.weighed, 1)
                    if kind == "stat" and key == "c":
                        if "B" not in index:
                            combine_rows()
                        pool.wait_ge(x_loaded, i * 16 + 16)
                        add(s.res[:], x_in[:], rows_over("bo_bg")).then_inc(s.summed, 1)
                    if kind == "norm" and key in ("x2", "x3", "cr", "x5", "x6", "x7"):
                        pool.wait_ge(*s.normed_at(i, key))
                        if key == "x2":
                            add(s.res[:], s.cur[:], rows_over("L0_b2")).then_inc(s.summed, 1)
                        elif key == "x3":
                            link(s, i, add(s.res[:], xl["x3"][:], rows_over("n2w"), ALU.mult))
                            link(s, i, add(s.res[:], s.res[:], rows_over("n2b_all")))
                        elif key == "cr":
                            link(s, i, add(cr[:], cr[:], rows_over("gamma2"), ALU.mult))
                            add(s.res[:], s.res[:], cr[:]).then_inc(s.summed, 1)
                        elif key == "x5":
                            link(s, i, add(s.res[:], xl["x5"][:], rows_over("L2_g"), ALU.mult))
                            add(s.res[:], s.res[:], rows_over("L2_b_b2")).then_inc(s.summed, 1)
                        elif key == "x6":
                            add(s.res[:], s.cur[:], rows_over("L3_bo")).then_inc(s.summed, 1)
                        elif key == "x7":
                            add(x7_all[:, bass.ds(i * PAIR, PAIR), :], s.cur[:], rows_over("b_prog"))\
                                .then_inc(s.summed, 1)
                assert all(linked[s] == POOL_LINKS[s] for s in index), linked

            turns(pool, turn)

        @block.vector
        def _(dve):
            def dense_ready(s, i, step):
                dve.wait_ge(*s.filled_at(i, *step))
                return s.dense_bank(step)

            def norm_io(s, key):
                return {"x": (x_in, s.xn, None), "c": (c_in, cn, None), "x2": (s.cur, s.xn, ("out", "L0")),
                        "x3": (s.cur, xl["x3"], ("ffn2", "L0")), "cr": (cr, cn, ("cross", "L1")),
                        "x5": (s.cur, xl["x5"], ("flip", "o")), "x6": (s.cur, s.xn, ("ffn2", "L2")),
                        "x7": (s.cur, s.xn, ("out", "L3"))}[key]

            def maximum(s, i, q):
                layer, b, c = QUADS[s.name][q]
                dve.wait_ge(s.scored, s.quads_at(i, q))
                dve.wait_ge(s.turned, s.quads_at(i, q) - PROBS + LEAD["probs"])
                nmx = s.nmx[:, q % PROBS, :]
                if layer in BIASED:
                    dve.sem_inc(dve_waited, 1)
                    for j in range(4):
                        more = bias[:, b, :] if layer == "L0" else causal[:]
                        ins = nc.vector.tensor_tensor_reduce(out=s.probs[:, q % PROBS, j, :],
                                                             in0=s.s_bank[:, j * P:j * P + P], in1=more,
                                                             scale=-1.0, scalar=3.0e38, op0=ALU.add, op1=ALU.min,
                                                             accum_out=nmx[:, j:j + 1])
                else:
                    n = PAIR if layer in ("L1a", "L1b") else 4
                    ins = nc.vector.tensor_reduce(nmx[:, 0:n], s.score_bank(q)[:, 0:n * P].rearrange("p (j k) -> p j k", j=n),
                                                  AX.X, ALU.max, negate=True)
                ins.then_inc(s.maxed, 1)

            dve.wait_ge(first_loaded, 16 * len(FIRST_LOADS))
            for name, by in (("L1_n2w", D ** -0.5), ("L1_n3w", D ** -0.25)):
                both = cols[:, COLS[name]:COLS[name] + 2 * DC]
                nc.vector.tensor_scalar(both, both, by, None, ALU.mult)
            for l, name in enumerate(("L0_bk", "L2_bk")):
                for h in range(2):
                    ins = nc.vector.tensor_scalar(bk_half[:, l, h, :], cols[:, COLS[name]:COLS[name] + DC],
                                                  masks[:, 8 + h:9 + h], None, ALU.mult)
            ins.then_inc(set_up_dve, 1)
            dve.wait_ge(set_up_dve, 1)

            def drive_weight():
                dve.wait_ge(set_up_pe, 1)
                nc.vector.tensor_copy(w_drive[:], Bs.o_bank[:, 0:DC * SS].rearrange("p (m s) -> p m s", m=DC))
                nc.vector.tensor_copy(b_drive[:], Bs.o_bank[0:SS, 128:129]).then_inc(set_up_dve, 1)
                dve.wait_ge(set_up_dve, 2)

            dve.wait_ge(set_up, 3)

            def turn(index):
                linked = {"A": 0, "B": 0, "H": 0}

                def link(s, i, ins):
                    linked[s.name] += 1
                    ins.then_inc(s.dve_link, 1)
                    dve.wait_ge(s.dve_link, i * DVE_LINKS[s.name] + linked[s.name])

                for s, i, step in live(index):
                    kind, key = step[0], step[1]
                    if kind == "stat":
                        src, _, ready = norm_io(s, key)
                        if key == "x":
                            dve.wait_ge(x_loaded, i * 16 + 16)
                        elif key == "c":
                            dve.wait_ge(c_loaded, i * 32 + 32)
                        else:
                            dve.wait_ge(*s.drained_at(i, *ready))
                        for b in range(PAIR):
                            ins = nc.vector.bn_stats(s.stats[:, b, :], src[:, b, :])
                        link(s, i, ins)
                        dve.sem_inc(dve_waited, 1)
                        for b in range(PAIR):
                            ins = nc.vector.bn_aggr(s.moments[:, b, :], s.stats[:, b, :])
                        link(s, i, ins)
                        nc.vector.tensor_scalar(s.veps[:], s.moments[:, :, 1], EPS, None, ALU.add)\
                            .then_inc(s.var_ready, 1)
                    elif kind == "norm":
                        src, dst, _ = norm_io(s, key)
                        dve.wait_ge(s.rstd_ready, i * len(STATS[s.name]) + STATS[s.name].index(key) + 1)
                        for b in range(PAIR):
                            nc.vector.tensor_scalar(dst[:, b, :], src[:, b, :], s.moments[:, b, 0:1],
                                                    s.rstd[:, b:b + 1], ALU.subtract, ALU.mult)\
                                .then_inc(s.normed, 1)
                        if key == "x":
                            dve.wait_ge(c_loaded, i * 32 + 32)
                            link(s, i, nc.vector.tensor_scalar(bias[:], bias[:], 1.0, -NEG, ALU.subtract, ALU.mult))
                    elif kind == "flip" and key in ("x", "x2", "x3", "cr", "x5", "x6", "x7"):
                        d = dense_ready(s, i, step)
                        g, b = {"x": ("L0_g1", "L0_be1"), "x2": ("L0_g2", "L0_be2"), "x3": ("L1_n2w", "L1_n2b"),
                                "cr": ("L1_n3w", "L1_n3b"), "x5": ("L2_g", "L2_b"), "x6": ("L3_g1", "L3_be1"),
                                "x7": ("L3_g2", "L3_be2")}[key]
                        for c in range(DC):
                            nc.vector.tensor_scalar(s.actT[:, c, :], d[:, c * PT:c * PT + PT], col(g, c), col(b, c),
                                                    ALU.mult, ALU.add)\
                                .then_inc(s.flipped if c == 0 else s.drained[bank_of(step)], 1)
                    elif kind == "flip" and key == "o":
                        d = dense_ready(s, i, step)
                        nc.vector.tensor_tensor(s.cur[:], by_batch(d), x4[:], ALU.add).then_inc(s.drained["d"], 1)
                    elif kind == "q":
                        dve.wait_ge(*s.drained_at(i, *step))
                        m0 = 4 if key == "L3" else 0
                        for c in range(DC):
                            for v in range(4):
                                ins = nc.vector.tensor_scalar(s.qm[:, v, c], s.oT[:, c], masks[:, m0 + v:m0 + v + 1],
                                                              None, ALU.mult)
                            ins.then_inc(s.masked, 1)
                    elif kind == "v" and key in ("L0", "L2"):
                        d = dense_ready(s, i, step)
                        heads = d[:].rearrange("p (b h e n) -> p b h e n", b=PAIR, h=H16 // 2, e=2)
                        for e, lo in ((0, 0), (1, 48)):
                            for b in range(PAIR):
                                ins = nc.vector.tensor_copy(s.vpad[:, b, :, lo:lo + 16], heads[:, b, :, e, :])
                        ins.then_inc(s.drained[bank_of(step)], 1)
                    elif kind == "score":
                        maximum(s, i, key)
                    elif kind == "sums":
                        dve.wait_ge(s.exped, s.quads_at(i, key) + LEAD["scores"])
                        n = PAIR if QUADS[s.name][key][0] in ("L1a", "L1b") else 4
                        nc.vector.reciprocal(s.rtotal[:, key % PROBS, 0:n], s.total[:, key % PROBS, 0:n])\
                            .then_inc(s.rsummed, 1)
                    elif kind == "turn":
                        dve.wait_ge(s.turned, s.quads_at(i, key) + LEAD["probs"])
                        dve.wait_ge(s.mixed, s.quads_at(i, key) - 2 + LEAD["mixed"])
                        n = PAIR if QUADS[s.name][key][0] in ("L1a", "L1b") else 4
                        nc.vector.tensor_copy(s.probsT[:, key % 2, 0:n, :],
                                              s.t_bank[:, 0:n * P].rearrange("p (j k) -> p j k", j=n))\
                            .then_inc(s.copied, 1)
                    elif kind == "mix" and QUADS[s.name][key][0] in HEADS_PER_LAYER:
                        layer, b, c = QUADS[s.name][key]
                        if 4 * (c + 1) == HEADS_PER_LAYER[layer]:
                            dve.wait_ge(s.mixed, s.quads_at(i, key) + LEAD["mixed"])
                            at = COLS[f"{layer}_bv"]
                            bv = cols[:, at:at + DC].unsqueeze(2).broadcast_to([P, DC, P])
                            nc.vector.tensor_tensor(s.oT[:, :, b * P:b * P + P],
                                                    s.o_bank[:, 0:DC * P].rearrange("p (c t) -> p c t", c=DC), bv,
                                                    ALU.add).then_inc(s.o_copied, 1)
                    elif kind in ("out", "ffn2"):
                        d = dense_ready(s, i, step)
                        job = {("out", "L0"): "xb", ("ffn2", "L0"): "x2b", ("ffn2", "L2"): "x5b",
                               ("out", "L3"): "x6b"}[kind, key]
                        dve.wait_ge(*s.summed_at(i, job))
                        nc.vector.tensor_tensor(s.cur[:], by_batch(d), s.res[:], ALU.add).then_inc(s.drained["d"], 1)
                    elif kind == "ffn1" and key == "L0":
                        d = dense_ready(s, i, step)
                        for m in range(2):
                            k = 2 * step[2] + m
                            ins = nc.vector.tensor_scalar(s.hT[:, k, :], d[:, m * PT:m * PT + PT], col("L0_b1", k),
                                                          0.0, ALU.add, ALU.max)
                        ins.then_inc(s.drained[bank_of(step)], 1)
                    elif kind == "self":
                        d = dense_ready(s, i, step)
                        link(s, i, nc.vector.tensor_tensor(s.cur[:], by_batch(d), rows_over("n3w"), ALU.mult))
                        dve.wait_ge(*s.summed_at(i, "skip"))
                        nc.vector.tensor_tensor(x4[:], s.cur[:], s.res[:], ALU.add).then_inc(s.drained["d"], 1)
                    elif kind == "drive":
                        d = dense_ready(s, i, step)
                        nc.vector.tensor_scalar(u_all[:, :, bass.ds(i * PAIR, PAIR)],
                                                d[0:SS, 0:PT].rearrange("p (b t) -> p t b", b=PAIR), b_drive[:], None,
                                                ALU.add).then_inc(s.drained["d"], 1)
                assert all(linked[s] == DVE_LINKS[s] for s in index), linked

            turns(dve, turn, drive_weight)

            dve.wait_ge(prog_meant, 1)
            nc.vector.tensor_copy(means[SS:P, :], Bs.o_bank[SS:P, 0:B]).then_inc(means_ready, 1)
            dve.wait_ge(means_ready, 1)
            nc.vector.tensor_copy(stT[SS:P, :, :], means[SS:P, :].unsqueeze(2).broadcast_to([SS, B, P]))\
                .then_inc(means_ready, 1)

            part = P // 4
            for t0 in range(0, P, part):
                dve.wait_ge(silued, t0 + part - 1)
                n = 4 if t0 == P - part else B
                for b in range(0, B, n):
                    ins = nc.vector.tensor_tensor(stT[0:SS, b:b + n, t0:t0 + part],
                                                  w_state[:, t0:t0 + part, b:b + n].rearrange("p t b -> p b t"),
                                                  u_all[:, t0:t0 + part, b:b + n].rearrange("p t b -> p b t"), ALU.add)
                    if n == 4:
                        ins.then_inc(states_ready, 1)
            dve.wait_ge(*Bs.summed_at(NT - 1, "x7b"))
            for n in range(B // PAIR):
                dve.wait_ge(last_filled, n + 1)
                x7 = x7_all[:, PAIR * n:PAIR * n + PAIR, :]
                nc.vector.tensor_tensor(x7, by_batch([Bs.s_bank, Bs.t_bank, Bs.d_bank][n % 3]), x7, ALU.add)\
                    .then_inc(last_added, 1)

        @block.scalar
        def _(act):
            def dense_ready(s, i, step):
                act.wait_ge(*s.filled_at(i, *step))
                return s.dense_bank(step)

            def turn(index):
                for s, i, step in live(index):
                    kind, key = step[0], step[1]
                    if kind == "score":
                        layer, b, c = QUADS[s.name][key]
                        act.wait_ge(s.maxed, s.quads_at(i, key) + LEAD["scores"])
                        slot = key % PROBS
                        for j in range(PAIR if layer in ("L1a", "L1b") else 4):
                            src = s.probs[:, slot, j, :] if layer in BIASED else s.score_bank(key)[:, j * P:j * P + P]
                            ins = nc.scalar.activation(s.probs[:, slot, j, :], src, ACT.Exp,
                                                       bias=s.nmx[:, slot, j:j + 1],
                                                       scale=-1.0 if layer in BIASED else 1.0,
                                                       accum_out=s.total[:, slot, j:j + 1])
                        ins.then_inc(s.exped, 1)
                    elif kind == "mix" and QUADS[s.name][key][0] == "L1a":
                        act.wait_ge(s.mixed, s.quads_at(i, key) + LEAD["mixed"])
                        nc.scalar.activation(h4[0:4, :], s.o_bank[0:4, 0:PT], ACT.Gelu, bias=fc1_b[:])\
                            .then_inc(s.o_copied, 1)
                    elif kind == "flip" and key in ("c", "x4"):
                        d = dense_ready(s, i, step)
                        nc.scalar.copy((cT if key == "c" else s.actT)[:], d[:].rearrange("p (c t) -> p c t", c=DC))\
                            .then_inc(s.drained["d"], 1)
                    elif kind == "flip" and key == "cn":
                        d = dense_ready(s, i, step)
                        for dst, g, b in ((n1T, "L1_n1w", "L1_n1b"), (n3T, "L3_g1", "L3_be1")):
                            for c in range(DC):
                                ins = nc.scalar.activation(dst[:, c, :], d[:, c * PT:c * PT + PT], ACT.Identity,
                                                           bias=col(b, c), scale=col(g, c))
                        ins.then_inc(s.drained[bank_of(step)], 1)
                    elif kind == "q":
                        d = dense_ready(s, i, step)
                        for c in range(DC):
                            ins = nc.scalar.activation(s.oT[:, c, :], d[:, c * PT:c * PT + PT], ACT.Identity,
                                                       bias=col(f"{key}_bq", c))
                        ins.then_inc(s.drained[bank_of(step)], 1)
                    elif kind == "k":
                        d = dense_ready(s, i, step)
                        for c in range(DC):
                            if key == "L3":
                                ins = nc.scalar.activation(k3T[:, c, :], d[:, c * PT:c * PT + PT], ACT.Identity,
                                                           bias=col("L3_bk", c))
                                continue
                            for h in range(2):
                                ins = nc.scalar.activation(s.kT[:, h, c, :], d[:, c * PT:c * PT + PT], ACT.Identity,
                                                           bias=bk_half[:, ("L0", "L2").index(key), h, c:c + 1],
                                                           scale=masks[:, 8 + h:9 + h])
                        ins.then_inc(s.drained[bank_of(step)], 1)
                    elif kind == "v" and key == "L1":
                        d = dense_ready(s, i, step)
                        nc.scalar.copy(v1[:], d[:, 0:4 * PAIR].rearrange("p (b n) -> p b n", b=PAIR))\
                            .then_inc(s.drained["d"], 1)
                    elif kind == "v" and key == "L3":
                        d = dense_ready(s, i, step)
                        nc.scalar.copy(v3[:], by_batch(d)).then_inc(s.drained["d"], 1)
                    elif kind == "cross":
                        d = dense_ready(s, i, step)
                        nc.scalar.copy(cr[:], by_batch(d)).then_inc(s.drained["d"], 1)
                    elif kind == "ffn1" and key == "L2":
                        d = dense_ready(s, i, step)
                        for m in range(2):
                            k = 2 * step[2] + m
                            ins = nc.scalar.activation(s.hT[:, k, :], d[:, m * PT:m * PT + PT], ACT.Gelu,
                                                       bias=col("L2_b1", k))
                        ins.then_inc(s.drained[bank_of(step)], 1)

            act.wait_ge(first_loaded, 16 * len(FIRST_LOADS))
            act.wait_ge(set_up_dve, 1)
            act.wait_ge(set_up, 3)
            turns(act, turn)

            z = [A.s_bank, A.t_bank, A.o_bank, A.d_bank]
            act.wait_ge(stepped, 1)
            nc.scalar.mul(w_state[:, 0, :], u_all[:, 0, :], 0.0)
            for t in range(1, P):
                act.wait_ge(stepped, t)
                nc.scalar.activation(w_state[:, t, :], z[t // 32][0:SS, (t % 32) * B:(t % 32) * B + B], ACT.Silu)\
                    .then_inc(silued, 1)


def _columns(inputs):
    import numpy as np
    n = lambda k: np.asarray(inputs[k])
    bqkv = n("L3_xattn_b_qkv")
    vecs = {"L0_g1": n("L0_xattn_g1"), "L0_be1": n("L0_xattn_be1"), "L0_bq": n("L0_xattn_bq"),
            "L0_bk": n("L0_xattn_bk"), "L0_bv": n("L0_xattn_bv"), "L0_g2": n("L0_xattn_g2"),
            "L0_be2": n("L0_xattn_be2"), "L0_b1": n("L0_xattn_b1"), "L1_n1w": n("L1_xattn_norm1_w"),
            "L1_n1b": n("L1_xattn_norm1_b"), "L1_n2w": n("L1_xattn_norm2_w"), "L1_n2b": n("L1_xattn_norm2_b"),
            "L1_n3w": n("L1_xattn_norm3_w"), "L1_n3b": n("L1_xattn_norm3_b"), "L2_bq": n("L2_xattn_bq"),
            "L2_bk": n("L2_xattn_bk"), "L2_bv": n("L2_xattn_bv"), "L2_b1": n("L2_xattn_b1"),
            "L2_g": n("L2_xattn_ln_g"), "L2_b": n("L2_xattn_ln_b"), "L3_g1": n("L3_xattn_g1"),
            "L3_be1": n("L3_xattn_beta1"), "L3_bq": bqkv[0:D], "L3_bk": bqkv[D:2 * D], "L3_bv": bqkv[2 * D:3 * D],
            "L3_g2": n("L3_xattn_g2"), "L3_be2": n("L3_xattn_beta2"), "L3_bin": n("L3_xattn_b_in")}
    return np.ascontiguousarray(np.concatenate([vecs[k].reshape(-1, P).T for k in COLS], axis=1))


def _arrays(inputs):
    import numpy as np
    n = lambda k: np.asarray(inputs[k])

    def lhs(w):
        return np.ascontiguousarray(w.T.reshape(-1, P, w.shape[0]).transpose(1, 0, 2))

    def rhs(w):
        return np.ascontiguousarray(w.reshape(-1, P, w.shape[1]).transpose(1, 0, 2))

    r = {"bo_bg": "L0_xattn_bo", "bg": "L0_xattn_bg", "L0_b2": "L0_xattn_b2", "n2w": "L1_xattn_norm2_w",
         "n2b_all": "L1_xattn_norm2_b", "gamma2": "L1_xattn_gamma2", "gamma1": "L1_xattn_gamma1",
         "n3w": "L1_xattn_norm3_w", "n3b": "L1_xattn_norm3_b", "L2_g": "L2_xattn_ln_g", "L2_b_b2": "L2_xattn_ln_b",
         "L2_b2": "L2_xattn_b2", "L3_bo": "L3_xattn_b_o", "b_prog": "L3_xattn_b_prog"}
    qkv = n("L3_xattn_W_qkv")
    part = np.arange(P)
    masks = np.zeros((P, 10), np.float32)
    for half in range(2):
        masks[part // 64 == half, 8 + half] = 1.0
    for v in range(4):
        masks[(part % 64) // 16 == v, v] = 16 ** -0.5
        masks[part // 32 == v, 4 + v] = 32 ** -0.5
    return {
        "x": n("x"), "ctx": n("ctx_1024"), "mask": n("mask_BxSxS2_fk0"), "prog": n("ctxb_2048x64"),
        "cols": _columns(inputs),
        "rows": np.ascontiguousarray(np.concatenate([n(r[k]) for k in ROWS])[None, :]),
        "ident": np.eye(P, dtype=np.float32), "masks": masks,
        "causal": np.where(np.tril(np.ones((P, P), bool)), 0.0, NEG).astype(np.float32),
        "L0_wq": lhs(n("L0_xattn_Wq")), "L0_wk": lhs(n("L0_xattn_Wk")), "L0_wv": lhs(n("L0_xattn_Wv")),
        "L0_wo": lhs(n("L0_xattn_Wo")), "L0_wg": lhs(n("L0_xattn_Wg")), "L0_w1": lhs(n("L0_xattn_W1")),
        "L0_w2": lhs(n("L0_xattn_W2")), "L1_fc1": lhs(n("L1_xattn_fc1_w")),
        "fc1_b": np.ascontiguousarray(n("L1_xattn_fc1_b")[:, None]),
        "fc2": np.ascontiguousarray(n("L1_xattn_fc2_w").T), "fc2_b": np.ascontiguousarray(n("L1_xattn_fc2_b")[None, :]),
        "L2_wq": lhs(n("L2_xattn_Wq")), "L2_wk": lhs(n("L2_xattn_Wk")), "L2_wv": lhs(n("L2_xattn_Wv")),
        "L2_w1": lhs(n("L2_xattn_W1")), "L2_w2": lhs(n("L2_xattn_W2")),
        "L3_wq": lhs(qkv[0:D]), "L3_wk": lhs(qkv[D:2 * D]), "L3_wv": lhs(qkv[2 * D:3 * D]),
        "L3_wo": lhs(n("L3_xattn_W_o")), "L3_w_in": rhs(n("L3_xattn_W_in")), "L3_bmat": rhs(n("L3_xattn_Bmat")),
        "a_t": np.ascontiguousarray(n("L3_xattn_A").T), "cmat": n("L3_xattn_Cmat"),
        "wprog": np.ascontiguousarray(n("L3_xattn_W_prog").T),
    }


def kernel(**inputs):
    import numpy as _np
    import concourse.bacc as _bacc
    from concourse.bass_utils import run_bass_kernel_spmd as _run

    nc = _bacc.Bacc("TRN2", target_bir_lowering=False, num_devices=1)
    arrays = {f"in_{k}": v for k, v in _arrays(inputs).items()}
    a = {k[3:]: nc.dram_tensor(k, v.shape, mybir.dt.from_np(v.dtype), kind="ExternalInput").ap()
         for k, v in arrays.items()}
    out = nc.dram_tensor("out_0", (B, P, D), F32, kind="ExternalOutput").ap()
    network(nc, a, out)
    r = _run(nc, [arrays], core_ids=[0])
    return r.results[0]["out_0"]
```
